# Optimizing a Trainium2 kernel written in Bass

```python
import numpy as np
import jax
import jax.numpy as jnp

def _softmax(x, axis=-1):
    return jax.nn.softmax(x, axis=axis)

def _gelu(x):
    return jax.nn.gelu(x, approximate=True)

def _silu(x):
    return jax.nn.silu(x)

def _sigmoid(x):
    return jax.nn.sigmoid(x)

def _layernorm(x, axis=-1, eps=1e-05):
    m = jnp.mean(x, axis=axis, keepdims=True)
    v = jnp.var(x, axis=axis, keepdims=True)
    return (x - m) / jnp.sqrt(v + eps)

def _scatter_add(tgt, idx, src, axis=0):
    return tgt.at[idx].add(src)

def _segment_sum(src, seg, n):
    return jax.ops.segment_sum(src, seg, n)
kernel_name = 'mk_prb_d1_jaxref_r8_b68d18'

def setup_inputs(seed: int=0):
    np.random.seed(seed)
    _w = jnp.asarray

    def _L0_attn_setup():
        import jax, jax.numpy as jnp
        import numpy as np
        INV_SQRT_M = 1.0 / np.sqrt(256.0).astype(np.float32)

        def _kernel_features(x, random_matrix):
            x_proj = jnp.einsum('bhsd,dm->bhsm', x, random_matrix)
            return (jax.nn.elu(x_proj) + 1.0) * INV_SQRT_M
        key = jax.random.key(seed)
        ks = jax.random.split(key, 7)
        B, S, D, H, M = (4, 512, 128, 16, 32)
        hd = D // H
        std = 1.0 / np.sqrt(D)
        return {'x': jax.random.normal(ks[0], (B, S, D), jnp.float32), 'Wq': jax.random.normal(ks[1], (D, D), jnp.float32) * std, 'bq': jnp.zeros((D,), jnp.float32), 'Wk': jax.random.normal(ks[2], (D, D), jnp.float32) * std, 'bk': jnp.zeros((D,), jnp.float32), 'Wv': jax.random.normal(ks[3], (D, D), jnp.float32) * std, 'bv': jnp.zeros((D,), jnp.float32), 'Wo': jax.random.normal(ks[4], (D, D), jnp.float32) * std, 'bo': jnp.zeros((D,), jnp.float32), 'random_matrix': jax.random.normal(ks[5], (hd, M), jnp.float32)}
    _L0_attn_in = _L0_attn_setup()

    def _L0_ffn_setup():
        import jax, jax.numpy as jnp
        import numpy as np
        D = 128
        H = 512
        O = 128
        E = 8
        K = 2
        key = jax.random.key(seed)
        ks = jax.random.split(key, 8)
        B, S = (2, 256)
        x = jax.random.normal(ks[0], (B, S, D), dtype=jnp.float32)
        s = 0.02
        Wr = jax.random.normal(ks[1], (D, E), dtype=jnp.float32) * s
        br = jnp.zeros((E,), dtype=jnp.float32)
        W1 = jax.random.normal(ks[2], (E, D, H), dtype=jnp.float32) * s
        b1 = jnp.zeros((E, H), dtype=jnp.float32)
        W2 = jax.random.normal(ks[3], (E, H, O), dtype=jnp.float32) * s
        b2 = jnp.zeros((E, O), dtype=jnp.float32)
        return {'x': x, 'Wr': Wr, 'br': br, 'W1': W1, 'b1': b1, 'W2': W2, 'b2': b2}
    _L0_ffn_in = _L0_ffn_setup()
    _d = {'L0_attn_x': _L0_attn_in['x'], 'L0_attn_Wq': _L0_attn_in['Wq'], 'L0_attn_bq': _L0_attn_in['bq'], 'L0_attn_Wk': _L0_attn_in['Wk'], 'L0_attn_bk': _L0_attn_in['bk'], 'L0_attn_Wv': _L0_attn_in['Wv'], 'L0_attn_bv': _L0_attn_in['bv'], 'L0_attn_Wo': _L0_attn_in['Wo'], 'L0_attn_bo': _L0_attn_in['bo'], 'L0_attn_random_matrix': _L0_attn_in['random_matrix'], 'L0_ffn_Wr': _L0_ffn_in['Wr'], 'L0_ffn_br': _L0_ffn_in['br'], 'L0_ffn_W1': _L0_ffn_in['W1'], 'L0_ffn_b1': _L0_ffn_in['b1'], 'L0_ffn_W2': _L0_ffn_in['W2'], 'L0_ffn_b2': _L0_ffn_in['b2']}
    _x0 = _d['L0_attn_x']
    _d['L0_attn_x'] = jax.random.normal(jax.random.fold_in(jax.random.key(seed), 1), (16, 256, 128), dtype=_x0.dtype)
    del _x0
    return _d

def reference(L0_attn_x, L0_attn_Wq, L0_attn_bq, L0_attn_Wk, L0_attn_bk, L0_attn_Wv, L0_attn_bv, L0_attn_Wo, L0_attn_bo, L0_attn_random_matrix, L0_ffn_Wr, L0_ffn_br, L0_ffn_W1, L0_ffn_b1, L0_ffn_W2, L0_ffn_b2):

    def _L0_attn_ref(x, Wq, bq, Wk, bk, Wv, bv, Wo, bo, random_matrix):
        import jax, jax.numpy as jnp
        import numpy as np
        INV_SQRT_M = 1.0 / np.sqrt(256.0).astype(np.float32)

        def _kernel_features(x, random_matrix):
            x_proj = jnp.einsum('bhsd,dm->bhsm', x, random_matrix)
            return (jax.nn.elu(x_proj) + 1.0) * INV_SQRT_M
        B, S, D = x.shape
        hd, M = random_matrix.shape
        H = D // hd
        q = (x @ Wq + bq).reshape(B, S, H, hd).transpose(0, 2, 1, 3)
        k = (x @ Wk + bk).reshape(B, S, H, hd).transpose(0, 2, 1, 3)
        v = (x @ Wv + bv).reshape(B, S, H, hd).transpose(0, 2, 1, 3)
        q_prime = _kernel_features(q, random_matrix)
        k_prime = _kernel_features(k, random_matrix)
        kv = jnp.einsum('bhsm,bhsd->bhmd', k_prime, v)
        k_sum = k_prime.sum(axis=2)
        out = jnp.einsum('bhsm,bhmd->bhsd', q_prime, kv)
        normalizer = jnp.einsum('bhsm,bhm->bhs', q_prime, k_sum)[..., None]
        normalizer = jnp.maximum(normalizer, 1e-06)
        out = out / normalizer
        out = out.transpose(0, 2, 1, 3).reshape(B, S, D)
        return out @ Wo + bo

    def _L0_ffn_ref(x, Wr, br, W1, b1, W2, b2):
        import jax, jax.numpy as jnp
        import numpy as np
        D = 128
        H = 512
        O = 128
        E = 8
        K = 2
        B, S, _ = x.shape
        T = B * S
        xf = x.reshape(T, D)
        logits = xf @ Wr + br
        topk_logits, topk_idx = jax.lax.top_k(logits, K)
        gates = jax.nn.softmax(topk_logits, axis=1)
        dense_gates = jnp.zeros((T, E), dtype=logits.dtype).at[jnp.arange(T)[:, None], topk_idx].set(gates)
        h = jax.nn.relu(jnp.einsum('td,edh->teh', xf, W1) + b1)
        y = jnp.einsum('teh,eho->teo', h, W2) + b2
        out = jnp.einsum('te,teo->to', dense_gates, y)
        return out.reshape(B, S, O)
    x = L0_attn_x
    xn = _layernorm(x, axis=-1)
    x = x + _L0_attn_ref(xn, L0_attn_Wq, L0_attn_bq, L0_attn_Wk, L0_attn_bk, L0_attn_Wv, L0_attn_bv, L0_attn_Wo, L0_attn_bo, L0_attn_random_matrix) + _L0_ffn_ref(xn, L0_ffn_Wr, L0_ffn_br, L0_ffn_W1, L0_ffn_b1, L0_ffn_W2, L0_ffn_b2)
    return x

_drawn_inputs = setup_inputs


def setup_inputs(seed=0):
    import zlib

    import numpy as np

    out = dict(_drawn_inputs(seed))
    spreads = {'L0_attn_bq': (0.0, 2.0),
     'L0_attn_bk': (0.0, 2.0),
     'L0_attn_bv': (0.0, 0.1),
     'L0_attn_bo': (0.0, 0.1),
     'L0_ffn_br': (0.0, 0.1),
     'L0_ffn_b1': (0.0, 0.382),
     'L0_ffn_b2': (0.0, 0.1)}
    factors = {'L0_attn_Wq': 3.366}
    for name, (base, spread) in spreads.items():
        noise = np.random.default_rng([zlib.crc32(name.encode()), seed]).standard_normal(out[name].shape)
        drawn = base * np.exp(spread * noise) if base else spread * noise
        out[name] = jnp.asarray(drawn.astype(out[name].dtype))
    for name, factor in factors.items():
        out[name] = (out[name] * factor).astype(out[name].dtype)
    return out
```

```python
import concourse.bass as bass
from concourse import mybir
from contextlib import ExitStack

P = 128
NBATCH = 16
NJ = 2
D = 128
NT = NBATCH * NJ
T = NT * P
HEADS, HD, M = 16, 8, 32
FEAT = HEADS * M
NC = FEAT // P
HC = P // M
KVW = HC * HD + HC
E, HID, TOPK = 8, 512, 2
HCH = HID // P
RT = 4
RG = NT // RT
MOE_TILES = -(-(TOPK * T + E * (P - 1)) // P)
MOE_TILES += MOE_TILES % 2
SLOTS = MOE_TILES * P
ROWW = D + 1
FIRST_LOAD = 10
PRE = 4
NO_ROW = TOPK * T
EPS = 1e-5
NORM_MIN = 1e-6 * 256.0
NEG = -3.0e38


def program(nc, x, wq, bq, wk, bk, wv, bv, wo, bo, rm, wr, br, w1, b1, w2, b2, out, rows_dram, y_dram):
    f32, f32r, f16, bf16 = mybir.dt.float32, mybir.dt.float32r, mybir.dt.float16, mybir.dt.bfloat16
    i32 = mybir.dt.int32
    ALU, ACT, AX = mybir.AluOpType, mybir.ActivationFunctionType, mybir.AxisListType
    ds = bass.ds

    with ExitStack() as ctx:
        def sb(name, shape, dt=f32):
            return ctx.enter_context(nc.sbuf_tensor(name, shape, dt))

        def sem(name):
            return ctx.enter_context(nc.semaphore(name))

        X = sb("X", [P, NT, D])
        SLOT_ROWS = sb("SLOT_ROWS", [P, MOE_TILES, ROWW])
        XS = SLOT_ROWS[:, 0:TOPK * NT, :].rearrange("p (k t) w -> p k t w", k=TOPK)
        YB = SLOT_ROWS[:, :, :].rearrange("p t w -> p (t w)")[:, 0:TOPK * NT * D].rearrange(
            "p (k t d) -> p k t d", k=TOPK, d=D)
        WRAW = sb("WRAW", [P, MOE_TILES * D])
        W1raw = WRAW[:, 0:E * HID].rearrange("p (e h) -> p e h", e=E)
        W2raw = WRAW[:, E * HID:2 * E * HID].rearrange("p (e h) -> p e h", e=E)
        YT = WRAW[:, :].rearrange("p (t d) -> p t d", d=D)
        W1h, W1l = sb("W1h", [P, E * HID], f16), sb("W1l", [P, E * HID], f16)
        W2h, W2l = sb("W2h", [P, E * HID], f16), sb("W2l", [P, E * HID], f16)
        PREFILL = sb("PREFILL", [P, PRE, ROWW])
        XN = sb("XN", [P, 2, RT, D])
        xT_hi, xT_lo = sb("xT_hi", [P, 2, NJ * P], f32r), sb("xT_lo", [P, 2, NJ * P], f32r)
        EK = sb("EK", [P, NJ, FEAT])
        KF = sb("KF", [P, 2, NJ, FEAT])
        EQ = sb("EQ", [P, NC, NJ * P])
        QF = sb("QF", [P, 2, NC, NJ * P])
        RB = EK[:, 0, :]
        WT = EK[:, 1, 0:2 * P]
        BQK = EK[:, 1, 2 * P:4 * P]
        XTR = EQ[:, :, :].rearrange("p c n -> p (c n)").rearrange("p (u n) -> p u n", u=2)
        KFflat = KF[:, :, :, :].rearrange("p a b c -> p (a b c)")
        QFflat = QF[:, :, :, :].rearrange("p a b c -> p (a b c)")
        NBIAS = 2 * FEAT + 2 * D
        B_REP = KFflat[:, 0:NBIAS]
        B_REST = QFflat[:, 0:NBIAS]
        B_PART = QFflat[:, NBIAS:NBIAS + NBIAS // 2].bitcast(bf16)
        ONEHOT = QFflat[:, 0:512].rearrange("p (e k t) -> p e k t", e=E, k=TOPK)
        ONEHOT16 = QFflat[:, 512:768].bitcast(bf16)
        CUM = QFflat[:, 768:1280]
        SLOTM = QFflat[:, 1280:1792]
        Hf = KF[:, 0, 0:2, :]
        Hs = KF[:, 1, 0:2, :].bitcast(f16).rearrange("p u (s n) -> p u s n", s=2)
        BIAS3 = sb("BIAS3", [P, NBIAS], bf16)
        WqR_hi, WqR_lo = sb("WqR_hi", [P, FEAT], f32r), sb("WqR_lo", [P, FEAT], f32r)
        WkR_hi, WkR_lo = sb("WkR_hi", [P, FEAT], f32r), sb("WkR_lo", [P, FEAT], f32r)
        Wv_hi, Wv_lo = sb("Wv_hi", [P, D], f32r), sb("Wv_lo", [P, D], f32r)
        Wq_sb, Wk_sb, Wv_sb, Wo_sb = (sb(n, [P, D]) for n in ("Wq_sb", "Wk_sb", "Wv_sb", "Wo_sb"))
        Wr_sb, br_sb = sb("Wr_sb", [P, E]), sb("br_sb", [P, E])
        R_sb = sb("R_sb", [P, M])
        bqk_sb = sb("bqk_sb", [P, 2])
        b1_sb, b1s = sb("b1_sb", [P, E * HCH]), sb("b1s", [P, E * HCH])
        b2_sb = sb("b2_sb", [P, E * D])
        ident, identh = sb("ident", [P, P]), sb("identh", [P, P], f16)
        upper = sb("upper", [P, P], bf16)
        ones = sb("ones", [P, 2 * P], bf16)
        ones32 = sb("ones32", [P, 512])
        head_mask = sb("head_mask", [P, HEADS])
        bd_mask = sb("bd_mask", [P, KVW])
        rank8 = sb("rank8", [P, E])
        tile_no = sb("tile_no", [P, MOE_TILES])
        stats = sb("stats", [P, NT, 6])
        ln = sb("ln", [P, 8, NT])
        mean, rstd = ln[:, 0, :], ln[:, 1, :]
        L, L2, EQM = sb("L", [P, NT, E]), sb("L2", [P, NT, E]), sb("EQM", [P, NT, E])
        top = sb("top", [P, TOPK, NT])
        best = sb("best", [P, TOPK, NT])
        gates = sb("gates", [P, TOPK, NT])
        gtmp = sb("gtmp", [P, NT])
        small = sb("small", [P, 16, E])
        smalli = sb("smalli", [P, 4, E], i32)
        slot_f, slot_i = sb("slot_f", [P, TOPK * NT]), sb("slot_i", [P, TOPK * NT], i32)
        cmp = sb("cmp", [P, MOE_TILES, E])
        expert_f, expert_i = sb("expert_f", [P, MOE_TILES]), sb("expert_i", [P, MOE_TILES], i32)
        VA = sb("VA", [P, 2, NJ, NC, KVW])
        BD = sb("BD", [P, NC, KVW])
        den = sb("den", [P, NJ * NC, HC])
        O_sb, OT_sb = sb("O_sb", [P, NJ * NC, HC * HD]), sb("OT_sb", [P, NJ * P])
        mx1, mx2, mx3 = sb("mx1", [P, 4]), sb("mx2", [P, 4]), sb("mx3", [P, 3])
        m3, m3b = sb("m3", [P, 1]), sb("m3b", [P, P])
        bound = sb("bound", [P, 2])
        fld, scl, inv = sb("fld", [P, 2], i32), sb("scl", [P, 2], i32), sb("inv", [P, 2], i32)
        c2 = sb("c2", [P, 1])
        neg1 = sb("neg1", [P, 1])
        XTS = sb("XTS", [P, 2, P])

        bank = [ctx.enter_context(nc.psum_tensor(f"bank{i}", [P, 512], f32)) for i in range(8)]
        psT, psOA, psK, psQ, psVK, psO = bank[0], bank[1], bank[2:4], bank[4:6], bank[6], bank[7]
        psV = psVK[:, 160:160 + NJ * D]
        psKV = psVK[:, 0:NC * KVW].rearrange("p (c w) -> p c w", c=NC)
        psOut = psO[:, 0:NJ * NC * KVW].rearrange("p (c w) -> p c w", w=KVW)

        s_early, s_x, s_late, s_w = sem("early_weights"), [sem(f"x_chunk{i}") for i in range(4)], sem("late_weights"), sem("expert_weights")
        s_const, s_pre, s_prefilled = sem("constants_made"), sem("prefill_made"), sem("slots_prefilled")
        s_wt, s_wtc, s_rb, s_bqk, s_fold, s_folded, s_vsplit, s_bias = (sem(n) for n in (
            "w_transposed", "w_transposed_copied", "rb_built", "bqk_repeated", "weights_folded",
            "weights_split_by_act", "weights_split_by_dve", "bias_parts_made"))
        s_var, s_sqrt = sem("variance_ready"), sem("sqrt_ready")
        s_pxn, s_phi, s_plo, s_pT, s_pxT, s_plog, s_pL = (sem(n) for n in (
            "router_rows_normalised", "router_hi_written", "router_lo_written", "router_transposed",
            "router_transposed_copied", "router_logits_done", "router_logits_read"))
        s_dup, s_ids = sem("rows_duplicated"), sem("row_numbers_written")
        s_gd, s_gexp, s_oneh, s_pfx, s_slots = (sem(n) for n in (
            "gate_difference", "gate_exp", "onehot_ready", "prefixes_done", "slots_ready"))
        s_scat = sem("rows_scattered")
        s_load = [sem("slots_loaded_first"), sem("slots_loaded_rest")]
        s_dve, s_pool, s_act = sem("dve_step"), sem("pool_step"), sem("act_step")
        (xn_ready, xt_done, xhi_ready, xlo_ready, k_done, v_done, q_done, ek_ready, kf_ready, eq_ready,
         qf_ready, v_ready, kv_done, bd_ready, out_done, o_ready, ot_done, ot_ready, att_done,
         base_ready) = (sem(n) for n in (
             "xn_ready", "xt_done", "xhi_ready", "xlo_ready", "k_done", "v_done", "q_done", "ek_ready",
             "kf_ready", "eq_ready", "qf_ready", "v_ready", "kv_done", "bd_ready", "out_done", "o_ready",
             "ot_done", "ot_ready", "att_done", "base_ready"))
        s_mx, s_mxT, s_m3, s_mb, s_scale, s_wsplit, s_whi = (sem(n) for n in (
            "weight_maxima", "maxima_transposed", "maxima_reduced", "maxima_broadcast", "scales_ready",
            "expert_weights_lo", "expert_weights_hi"))
        (m_T, m_xT, m_up, m_h, m_split, m_down, m_y) = (sem(n) for n in (
            "slot_rows_transposed", "slot_rows_copied", "up_done", "hidden_ready", "hidden_split",
            "down_done", "y_ready"))
        s_mread = sem("maxima_read")
        s_ysc = sem("y_scattered")
        s_yb = [sem(f"y_back{i}") for i in range(4)]
        s_fin, s_comb, s_norm, s_hi16 = sem("chunk_combined"), sem("tile_combined"), sem("norm_step"), sem("hidden_hi")
        s_out = sem("out_written")

        block = ctx.enter_context(nc.Block())
        FC = NT // 4

        def wait(eng, semaphore, value):
            if not isinstance(value, int) or value > 0:
                eng.wait_ge(semaphore, value)

        def spread(ap, dim, n):
            return ap.broadcast_to([n if i == dim else size for i, size in enumerate(ap.shape)])

        def live(b, n=NBATCH):
            return not isinstance(b, int) or 0 <= b < n

        def steps(eng, first, last, body):
            with eng.Fori(first, last, 2) as b:
                body(b, first % 2)
                body(b + 1, (first + 1) % 2)

        def x_view(dram):
            return dram.rearrange("b (p j) d -> p b j d", j=NJ)

        @block.sync
        def _(sp):
            for dst, src in ((Wq_sb[:], wq), (Wk_sb[:], wk), (bqk_sb[:, 0:1], bq.unsqueeze(1)),
                             (bqk_sb[:, 1:2], bk.unsqueeze(1)), (Wv_sb[:], wv)):
                sp.dma_start(dst, src).then_inc(s_early, 16)
            for g in range(4):
                sp.dma_start(X[:, FC * g:FC * (g + 1), :].rearrange("p (b j) d -> p b j d", j=NJ),
                             x_view(x)[:, g * FC // NJ:(g + 1) * FC // NJ]).then_inc(s_x[g], 16)
            sp.wait_ge(s_pre, 1)
            pre = rows_dram.rearrange("(g p t) w -> g p t w", p=P, t=PRE)
            for g in range(MOE_TILES // PRE):
                sp.dma_start(pre[g], PREFILL[:]).then_inc(s_prefilled, 16)
            sp.dma_start(W1raw, w1.rearrange("e d h -> d e h")).then_inc(s_w, 16)
            sp.dma_start(W2raw.rearrange("p e (c o) -> p e c o", c=HCH),
                         w2.rearrange("e (p c) o -> p e c o", c=HCH)).then_inc(s_w, 16)
            sp.wait_ge(s_scat, 16 * TOPK * NT)
            slots = rows_dram.rearrange("(t p) w -> p t w", p=P)
            sp.dma_start(SLOT_ROWS[:, 0:FIRST_LOAD, :], slots[:, 0:FIRST_LOAD]).then_inc(s_load[0], 16)
            sp.dma_start(SLOT_ROWS[:, FIRST_LOAD:, :], slots[:, FIRST_LOAD:]).then_inc(s_load[1], 16)
            sp.wait_ge(s_ysc, 16 * MOE_TILES)
            yv = y_dram.rearrange("(k p t) d -> p k t d", k=TOPK, p=P)
            for g in range(4):
                for k in range(TOPK):
                    sp.dma_start(YB[:, k, FC * g:FC * (g + 1), :], yv[:, k, FC * g:FC * (g + 1)]).then_inc(s_yb[g], 16)
            for g in range(4):
                sp.wait_ge(s_fin, g + 1)
                sp.dma_start(x_view(out)[:, g * FC // NJ:(g + 1) * FC // NJ],
                             X[:, FC * g:FC * (g + 1), :].rearrange("p (b j) d -> p b j d", j=NJ)).then_inc(s_out, 16)
            sp.wait_ge(s_out, 64)

        @block.gpsimd
        def _(pool):
            count = [0]

            def link(ins):
                count[0] += 1
                ins.then_inc(s_pool, 1)
                pool.wait_ge(s_pool, count[0])

            def keep(t, op, base, pattern, mult):
                link(nc.gpsimd.affine_select(out=t, in_=t, compare_op=op, fill=0.0, base=base,
                                             pattern=pattern, channel_multiplier=mult))

            for t in (ident, upper, ones, ones32, bd_mask, head_mask, VA):
                nc.gpsimd.memset(t[:], 1.0)
            link(nc.gpsimd.memset(PREFILL[:], 0.0))
            nc.gpsimd.memset(PREFILL[:].bitcast(i32)[:, :, D], NO_ROW).then_inc(s_pre, 1)
            keep(ident[:], ALU.is_equal, 0, [[1, P]], -1)
            link(nc.gpsimd.tensor_copy(identh[:], ident[:]))
            keep(head_mask[:], ALU.is_ge, 0, [[-HD, HEADS]], 1)
            keep(head_mask[:], ALU.is_ge, HD - 1, [[HD, HEADS]], -1)
            for v, inner in ((bd_mask[:, 0:HC * HD], [[0, HD]]), (bd_mask[:, HC * HD:KVW], [])):
                keep(v, ALU.is_ge, 0, [[-M, HC]] + inner, 1)
                keep(v, ALU.is_ge, M - 1, [[M, HC]] + inner, -1)
            keep(upper[:], ALU.is_gt, 0, [[1, P]], -1)
            nc.gpsimd.iota(rank8[:], pattern=[[-1, E]], base=E, channel_multiplier=0,
                           allow_small_or_imprecise_dtypes=True)
            link(nc.gpsimd.iota(tile_no[:], pattern=[[1, MOE_TILES]], base=0, channel_multiplier=0,
                                allow_small_or_imprecise_dtypes=True))
            nc.gpsimd.iota(XS.bitcast(i32)[:, :, :, D], pattern=[[T, TOPK], [1, NT]], base=0,
                           channel_multiplier=NT).then_inc(s_const, 1)

            def dup(g, u):
                pool.wait_ge(s_plo, g + 1)
                pool.wait_ge(s_phi, g + 1)
                nc.gpsimd.tensor_copy(XS[:, 1, ds(g * RT, RT), 0:D], XS[:, 0, ds(g * RT, RT), 0:D]).then_inc(s_dup, 1)
            steps(pool, 0, RG - 1, dup)
            pool.wait_ge(s_dup, RG)
            pool.wait_ge(s_slots, 1)
            pool.wait_ge(s_prefilled, 16 * (MOE_TILES // PRE))
            for c in range(TOPK * NT):
                nc.gpsimd.indirect_dma_start(
                    rows_dram, bass.IndirectOffsetOnAxis(ap=slot_i[:, c:c + 1], axis=0),
                    XS[:, c // NT, c % NT, :], None).then_inc(s_scat, 16)
            ids = SLOT_ROWS[:].bitcast(i32)
            pool.wait_ge(s_load[0], 16)
            for t in range(MOE_TILES):
                if t == FIRST_LOAD:
                    pool.wait_ge(s_load[1], 16)
                pool.wait_ge(m_y, t + 1)
                nc.gpsimd.indirect_dma_start(
                    y_dram, bass.IndirectOffsetOnAxis(ap=ids[:, t, D:D + 1], axis=0), YT[:, t, :], None,
                    bounds_check=NO_ROW - 1, oob_is_err=False).then_inc(s_ysc, 16)

        @block.scalar
        def _(act):
            act.dma_start(R_sb[:], bass.AP(rm.tensor, 0, [[0, P // HD], [M, HD], [1, M]])).then_inc(s_early, 16)
            act.dma_start(B_REP[:, 2 * FEAT:2 * FEAT + D], bv.partition_broadcast(P)).then_inc(s_early, 16)
            act.dma_start(B_REP[:, 2 * FEAT + D:NBIAS], bo.partition_broadcast(P)).then_inc(s_early, 16)
            act.dma_start(Wr_sb[:], wr).then_inc(s_late, 16)
            act.dma_start(br_sb[:], br.partition_broadcast(P)).then_inc(s_late, 16)
            act.dma_start(Wo_sb[:], wo).then_inc(s_late, 16)
            act.dma_start(b1_sb[:].rearrange("p (e c) -> p e c", e=E), b1.rearrange("e (p c) -> p e c", c=HCH)).then_inc(s_late, 16)
            act.dma_start(b2_sb[:], b2.rearrange("e o -> (e o)").partition_broadcast(P)).then_inc(s_late, 16)

            act.wait_ge(s_wt, 1)
            nc.scalar.copy(WT, bank[0][:, 0:2 * P]).then_inc(s_wtc, 1)
            act.wait_ge(s_fold, 1)
            nc.scalar.copy(WqR_hi[:], bank[1][:])
            nc.scalar.copy(WkR_hi[:], bank[2][:])
            act.wait_ge(s_early, 16 * 8)
            nc.scalar.copy(Wv_hi[:], Wv_sb[:]).then_inc(s_folded, 1)
            act.wait_ge(s_var, 1)
            nc.scalar.activation(ln[:, 3, :], ln[:, 2, :], ACT.Sqrt).then_inc(s_sqrt, 1)

            def router(g, u):
                act.wait_ge(s_pxn, g + 1)
                nc.scalar.copy(XS[:, 0, ds(g * RT, RT), 0:D // 2].bitcast(f16), XN[:, u]).then_inc(s_phi, 1)
                act.wait_ge(s_pT, g + 1)
                wait(act, s_plog, g - 1)
                nc.scalar.copy(XTR[:, u, :], bank[u][:]).then_inc(s_pxT, 1)
            router(0, 0)
            router(1, 1)
            steps(act, 2, RG - 1, router)
            act.wait_ge(s_gd, 1)
            nc.scalar.activation(gtmp[:], gtmp[:], ACT.Exp).then_inc(s_gexp, 1)

            def hi_part(b):
                if not live(b):
                    return
                u = parity(b)
                act.wait_ge(xt_done, b + 1)
                wait(act, q_done, 2 * b - 2)
                nc.scalar.copy(xT_hi[:, u, :], psT[:, 0:NJ * P]).then_inc(xhi_ready, 1)

            par = [0]

            def parity(b):
                return b % 2 if isinstance(b, int) else par[0]

            def step(b, u, weights=None):
                par[0] = 1 - u
                hi_part(b + 1)
                par[0] = u
                if live(b):
                    for j in range(NJ):
                        act.wait_ge(k_done, 2 * b + j + 1)
                        wait(act, kf_ready, 2 * b - 1 + j)
                        nc.scalar.activation(EK[:, j, :], psK[j][:], ACT.Exp, bias=neg1[:, 0:1]).then_inc(ek_ready, 1)
                        if j == 0 and live(b - 2):
                            act.wait_ge(ot_done, b - 1)
                            wait(act, att_done, b - 2)
                            nc.scalar.copy(OT_sb[:], psOA[:, 0:NJ * P]).then_inc(ot_ready, 1)
                    act.wait_ge(v_done, b + 1)
                    wait(act, kv_done, b - 1)
                    nc.scalar.copy(VA[:, u, :, :, 0:HC * HD],
                                   psV.rearrange("p (j c w) -> p j c w", j=NJ, c=NC)).then_inc(v_ready, 1)
                    for h in range(2):
                        act.wait_ge(q_done, 2 * b + h + 1)
                        wait(act, qf_ready, 2 * b - 1 + h)
                        nc.scalar.activation(EQ[:, 2 * h:2 * h + 2, :].rearrange("p c n -> p (c n)"), psQ[h][:],
                                             ACT.Exp, bias=neg1[:, 0:1]).then_inc(eq_ready, 1)
                elif live(b - 2):
                    act.wait_ge(ot_done, b - 1)
                    act.wait_ge(att_done, b - 2)
                    nc.scalar.copy(OT_sb[:], psOA[:, 0:NJ * P]).then_inc(ot_ready, 1)
                if weights is not None:
                    for raw, hi, s in ((W1raw[:, ds(weights, 1), :].rearrange("p e (a c) -> p (e c) a", c=HCH), W1h, 0),
                                       (W2raw[:, ds(weights, 1), :].rearrange("p e (c a) -> p (e c) a", c=HCH), W2h, 1)):
                        last = nc.scalar.activation(hi[:, ds(weights * HID, HID)].rearrange("p (c a) -> p c a", c=HCH), raw,
                                                    ACT.Copy, scale=scl[:].bitcast(f32)[:, s:s + 1])
                    last.then_inc(s_whi, 1)

            act.wait_ge(s_const, 1)
            for b in (-1, 0, 1, 2):
                step(b, b % 2)
            steps(act, 3, 6, step)
            step(7, 1)
            act.wait_ge(s_scale, 1)
            with act.Fori(8, 13, 2) as b:
                step(b, 0, b - 8)
                step(b + 1, 1, b - 7)
            for b, e in ((14, 6), (15, 7), (16, None), (17, None)):
                step(b, b % 2, e)

            def copy_rows(t, u):
                act.wait_ge(m_T, t + 1)
                wait(act, m_up, t - 1)
                nc.scalar.copy(XTS[:, u, :], bank[u][:, 0:P]).then_inc(m_xT, 1)

            def moe(t, u):
                if live(t + 1, MOE_TILES):
                    copy_rows(t + 1, 1 - u)
                e = act.value_load(expert_i[0:1, ds(t, 1)], min_val=0, max_val=E - 1)
                act.wait_ge(m_up, t + 1)
                wait(act, m_split, t - 1)
                for c in range(HCH):
                    last = nc.scalar.activation(Hf[:, u, c * P:(c + 1) * P], bank[2 + u][:, c * P:(c + 1) * P],
                                                ACT.Relu, bias=b1s[:, ds(e * HCH + c, 1)])
                last.then_inc(m_h, 1)
            copy_rows(0, 0)
            for t in range(3):
                moe(t, t % 2)
            steps(act, 3, MOE_TILES - 2, moe)
            moe(MOE_TILES - 1, 1)

        @block.vector
        def _(dve):
            count = [0]

            def link(ins):
                count[0] += 1
                ins.then_inc(s_dve, 1)
                dve.wait_ge(s_dve, count[0])

            V = nc.vector
            nc.vector.memset(neg1[:], -1.0)
            link(V.memset(BIAS3[:], 0.0))
            dve.wait_ge(s_early, 16 * 8)
            dve.wait_ge(s_const, 1)
            V.tensor_tensor(RB.rearrange("p (h m) -> p h m", h=HEADS), spread(R_sb[:].unsqueeze(1), 1, HEADS),
                            spread(head_mask[:].unsqueeze(2), 2, M), ALU.mult).then_inc(s_rb, 1)
            V.tensor_copy(BQK.rearrange("p (a n) -> p a n", a=2),
                          spread(bqk_sb[:].unsqueeze(2), 2, P)).then_inc(s_bqk, 1)
            dve.wait_ge(s_fold, 1)
            V.tensor_scalar(B_REP[:, 0:FEAT], bank[3][:], 1.0, None, ALU.add)
            V.tensor_scalar(B_REP[:, FEAT:2 * FEAT], bank[4][:], 1.0, None, ALU.add)
            dve.wait_ge(s_folded, 1)
            V.tensor_tensor(WqR_lo[:], bank[1][:], WqR_hi[:].bitcast(f32), ALU.subtract)
            V.tensor_tensor(WkR_lo[:], bank[2][:], WkR_hi[:].bitcast(f32), ALU.subtract)
            link(V.tensor_tensor(Wv_lo[:], Wv_sb[:], Wv_hi[:].bitcast(f32), ALU.subtract))
            link(V.tensor_copy(B_PART, B_REP))
            V.tensor_copy(BIAS3[0:1, :], B_PART[0:1, :])
            link(V.tensor_tensor(B_REST, B_REP, B_PART, ALU.subtract))
            link(V.tensor_copy(B_PART, B_REST))
            V.tensor_copy(BIAS3[32:33, :], B_PART[32:33, :])
            link(V.tensor_tensor(B_REST, B_REST, B_PART, ALU.subtract))
            V.tensor_copy(BIAS3[64:65, :], B_REST[64:65, :]).then_inc(s_bias, 1)

            for g in range(4):
                dve.wait_ge(s_x[g], 16)
                with dve.Fori(FC * g, FC * (g + 1)) as t:
                    last = V.bn_stats(stats[:, ds(t, 1), :].rearrange("p a s -> p (a s)"),
                                      X[:, ds(t, 1), :].rearrange("p a d -> p (a d)"))
            link(V.memset(small[:], 0.0))
            me, se, mo, so = stats[:, :, 1], stats[:, :, 2], stats[:, :, 4], stats[:, :, 5]
            a, v, y, z = ln[:, 4, :], ln[:, 2, :], ln[:, 5, :], ln[:, 6, :]
            V.tensor_tensor(a, me, mo, ALU.add)
            V.tensor_tensor(y, me, mo, ALU.subtract)
            link(V.tensor_tensor(v, se, so, ALU.add))
            V.tensor_scalar(mean, a, 0.5, None, ALU.mult)
            link(V.scalar_tensor_tensor(y, y, 0.25, y, ALU.mult, ALU.mult))
            link(V.scalar_tensor_tensor(v, v, 1.0 / D, y, ALU.mult, ALU.add))
            V.tensor_scalar(v, v, EPS, None, ALU.add).then_inc(s_var, 1)
            dve.wait_ge(s_sqrt, 1)
            link(V.reciprocal(y, ln[:, 3, :]))
            link(V.tensor_tensor(z, y, y, ALU.mult))
            link(V.tensor_tensor(z, z, v, ALU.mult))
            link(V.tensor_scalar(z, z, -0.5, 1.5, ALU.mult, ALU.add))
            link(V.tensor_tensor(rstd, y, z, ALU.mult))

            def normalise(tile, dst):
                return V.tensor_scalar(dst, X[:, ds(tile, 1), :].rearrange("p a d -> p (a d)"),
                                       mean[:, ds(tile, 1)], rstd[:, ds(tile, 1)], ALU.subtract, ALU.mult)

            def logits(g, u):
                dve.wait_ge(s_plog, g + 1)
                V.tensor_tensor(L[:, ds(g * RT, RT), :], bank[2 + u][:, 0:RT * E].rearrange("p (t e) -> p t e", e=E),
                                spread(br_sb[:].unsqueeze(1), 1, RT), ALU.add).then_inc(s_pL, 1)

            def router(g, u):
                wait(dve, s_pT, g - 1)
                wait(dve, s_phi, g - 1)
                for i in range(RT):
                    last = normalise(g * RT + i, XN[:, u, i, :])
                last.then_inc(s_pxn, 1)
                dve.wait_ge(s_phi, g + 1)
                dve.wait_ge(s_pxn, g + 1)
                V.tensor_tensor(XS[:, 0, ds(g * RT, RT), D // 2:D].bitcast(f16), XN[:, u],
                                XS[:, 0, ds(g * RT, RT), 0:D // 2].bitcast(f16), ALU.subtract).then_inc(s_plo, 1)
                if live(g - 1):
                    logits(g - 1, 1 - u)
            dve.wait_ge(s_late, 16 * 5)
            router(0, 0)
            router(1, 1)
            steps(dve, 2, RG - 1, router)
            logits(RG - 1, (RG - 1) % 2)
            dve.wait_ge(s_pL, RG)

            def bc_e(t):
                return spread(t.unsqueeze(2), 2, E)
            rank_b = spread(rank8[:].unsqueeze(1), 1, NT)
            src = L
            for k in range(TOPK):
                link(V.tensor_reduce(top[:, k, :], src[:], AX.X, ALU.max))
                link(V.tensor_tensor(EQM[:], src[:], bc_e(top[:, k, :]), ALU.is_equal))
                link(V.tensor_tensor(EQM[:], EQM[:], rank_b, ALU.mult))
                link(V.tensor_reduce(best[:, k, :], EQM[:], AX.X, ALU.max))
                oh = ONEHOT[:, :, k, :].rearrange("p e t -> p t e")
                link(V.tensor_tensor(oh, bc_e(best[:, k, :]), rank_b, ALU.is_equal))
                if k == 0:
                    link(V.scalar_tensor_tensor(L2[:], oh, NEG, L[:], ALU.mult, ALU.add))
                    src = L2
            ohf = ONEHOT.rearrange("p e k t -> p (e k t)")
            V.tensor_copy(ONEHOT16, ohf).then_inc(s_oneh, 1)
            V.tensor_tensor(gtmp[:], top[:, 1, :], top[:, 0, :], ALU.subtract).then_inc(s_gd, 1)
            dve.wait_ge(s_pfx, 1)
            TOT, PFX = bank[1], bank[0]
            link(V.tensor_tensor_scan(CUM, ones32[:], TOT[:], 0.0, ALU.mult, ALU.add))
            cume = CUM.rearrange("p (e n) -> p e n", e=E)
            cinc, n, ntile, tinc, tf, cex, delta = (small[:, i, :] for i in range(7))
            V.tensor_copy(cinc, cume[:, :, TOPK * NT - 1])
            link(V.memset(cex[:, 0:1], 0.0))
            link(V.tensor_copy(cex[:, 1:E], cinc[:, 0:E - 1]))
            link(V.tensor_tensor(n, cinc, cex, ALU.subtract))
            link(V.tensor_scalar(smalli[:, 0, :], n, float(P - 1), None, ALU.add))
            link(V.tensor_scalar(smalli[:, 1, :], smalli[:, 0, :], 7, None, ALU.logical_shift_right))
            link(V.tensor_copy(ntile, smalli[:, 1, :]))
            link(V.tensor_tensor_scan(tinc, ones32[:, 0:E], ntile, 0.0, ALU.mult, ALU.add))
            link(V.tensor_tensor(tf, tinc, ntile, ALU.subtract))
            link(V.scalar_tensor_tensor(delta, tf, float(P), cex, ALU.mult, ALU.subtract))
            link(V.tensor_tensor(SLOTM, CUM, TOT[:], ALU.subtract))
            link(V.tensor_tensor(SLOTM, SLOTM, PFX[:], ALU.add))
            sl = SLOTM.rearrange("p (e n) -> p e n", e=E)
            link(V.tensor_tensor(sl, sl, spread(delta.unsqueeze(2), 2, TOPK * NT), ALU.add))
            link(V.tensor_tensor(SLOTM, SLOTM, ohf, ALU.mult))
            link(V.tensor_reduce(slot_f[:], SLOTM.rearrange("p (e n) -> p n e", e=E), AX.X, ALU.add))
            V.tensor_copy(slot_i[:], slot_f[:]).then_inc(s_slots, 1)
            link(V.tensor_tensor(cmp[:], spread(tile_no[:].unsqueeze(2), 2, E),
                                 spread(tinc.unsqueeze(1), 1, MOE_TILES), ALU.is_ge))
            link(V.tensor_reduce(expert_f[:], cmp[:], AX.X, ALU.add))
            link(V.tensor_scalar(expert_i[:], expert_f[:], float(E - 1), None, ALU.min))
            dve.wait_ge(s_gexp, 1)
            link(V.tensor_scalar(best[:, 0, :], gtmp[:], 1.0, None, ALU.add))
            link(V.reciprocal(gates[:, 0, :], best[:, 0, :]))
            link(V.tensor_tensor(gates[:, 1, :], gates[:, 0, :], gtmp[:], ALU.mult))

            par = [0]

            def parity(b):
                return b % 2 if isinstance(b, int) else par[0]

            def rows(b):
                if live(b):
                    wait(dve, xt_done, b - 1)
                    for j in range(NJ):
                        last = normalise(b * NJ + j, XN[:, parity(b), j, :])
                    last.then_inc(xn_ready, 1)

            def lo_part(b):
                if live(b):
                    u = parity(b)
                    dve.wait_ge(xhi_ready, b + 1)
                    V.tensor_tensor(xT_lo[:, u, :], psT[:, 0:NJ * P], xT_hi[:, u, :].bitcast(f32),
                                    ALU.subtract).then_inc(xlo_ready, 1)

            def step(b, u, maxima=None, weights=None, hooks=None):
                par[0] = u
                rows(b + 2)
                par[0] = 1 - u
                lo_part(b + 1)
                par[0] = u
                if hooks:
                    hooks[0]()
                if live(b - 1):
                    dve.wait_ge(kv_done, b)
                    wait(dve, out_done, b - 1)
                    V.tensor_tensor(BD[:], psKV, spread(bd_mask[:].unsqueeze(1), 1, NC), ALU.mult).then_inc(bd_ready, 1)
                if live(b):
                    for j in range(NJ):
                        dve.wait_ge(ek_ready, 2 * b + j + 1)
                        wait(dve, kv_done, b - 1)
                        V.scalar_tensor_tensor(KF[:, u, j, :], EK[:, j, :], 1.0, psK[j][:], ALU.min, ALU.max).then_inc(kf_ready, 1)
                        if hooks and j == 0:
                            hooks[1]()
                    for h in range(2):
                        dve.wait_ge(eq_ready, 2 * b + h + 1)
                        wait(dve, out_done, b - 1)
                        V.scalar_tensor_tensor(QF[:, u, 2 * h:2 * h + 2, :].rearrange("p c n -> p (c n)"),
                                               EQ[:, 2 * h:2 * h + 2, :].rearrange("p c n -> p (c n)"), 1.0,
                                               psQ[h][:], ALU.min, ALU.max).then_inc(qf_ready, 1)
                        if hooks and h == 0:
                            hooks[2]()
                if live(b - 2):
                    dve.wait_ge(att_done, b - 1)
                    xb = X[:, ds((b - 2) * NJ, NJ), :]
                    V.tensor_tensor(xb, psOA[:, NJ * P:2 * NJ * P].rearrange("p (j d) -> p j d", j=NJ), xb,
                                    ALU.add).then_inc(base_ready, 1)
                if live(b - 1):
                    dve.wait_ge(out_done, b)
                    link2(V.tensor_scalar(den[:], psOut[:, :, HC * HD:KVW], NORM_MIN, None, ALU.max), b)
                    link2(V.reciprocal(den[:], den[:]), b)
                    wait(dve, ot_done, b - 1)
                    V.tensor_tensor(O_sb[:].rearrange("p c (h d) -> p c h d", h=HC),
                                    psOut[:, :, 0:HC * HD].rearrange("p c (h d) -> p c h d", h=HC),
                                    spread(den[:].unsqueeze(3), 3, HD), ALU.mult).then_inc(o_ready, 1)
                if maxima is not None:
                    for raw, m in ((W1raw, mx1), (W2raw, mx2)):
                        V.tensor_reduce(m[:, ds(maxima, 1)], raw[:, ds(maxima * 2, 2), :].rearrange("p e h -> p (e h)"), AX.X, ALU.max,
                                        apply_absolute_value=True)
                if weights is not None:
                    dve.wait_ge(s_whi, weights + 1)
                    for raw, hi, lo, s in (
                            (W1raw[:, ds(weights, 1), :].rearrange("p e (a c) -> p (e c) a", c=HCH), W1h, W1l, 0),
                            (W2raw[:, ds(weights, 1), :].rearrange("p e (c a) -> p (e c) a", c=HCH), W2h, W2l, 1)):
                        at = ds(weights * HID, HID)
                        last = V.scalar_tensor_tensor(lo[:, at].rearrange("p (c a) -> p c a", c=HCH), raw,
                                                      scl[:].bitcast(f32)[:, s:s + 1],
                                                      hi[:, at].rearrange("p (c a) -> p c a", c=HCH), ALU.mult, ALU.subtract)
                    last.then_inc(s_wsplit, 1)

            def link2(ins, b):
                norm_half[0] ^= 1
                ins.then_inc(s_norm, 1)
                dve.wait_ge(s_norm, 2 * b - norm_half[0])
            norm_half = [0]

            def maxima_local():
                V.tensor_reduce(mx3[:, 0:1], mx1[:], AX.X, ALU.max)
                V.tensor_reduce(mx3[:, 1:2], mx2[:], AX.X, ALU.max)
                V.tensor_reduce(mx3[:, 2:3], b1_sb[:], AX.X, ALU.max, apply_absolute_value=True).then_inc(s_mx, 1)

            def maxima_reduced():
                dve.wait_ge(s_mxT, 1)
                link(V.tensor_reduce(m3[0:3, :], psO[0:3, 384:512], AX.X, ALU.max))
                V.tensor_copy(m3b[0:3, :], spread(m3[0:3, 0:1], 1, P)).then_inc(s_m3, 1)

            def scales():
                dve.wait_ge(s_mb, 1)
                V.tensor_copy(bound[:, 1:2], psO[:, 321:322])
                link(V.tensor_copy(c2[:], psO[:, 322:323]))
                V.scalar_tensor_tensor(bound[:, 0:1], psO[:, 320:321], float(D), c2[:], ALU.mult, ALU.add).then_inc(s_mread, 1)
                dve.wait_ge(s_mread, 1)
                link(V.tensor_scalar(fld[:], bound[:].bitcast(i32), 23, None, ALU.logical_shift_right))
                link(V.tensor_scalar(fld[:], fld[:], -1.0, 268.0, ALU.mult, ALU.add))
                link(V.tensor_scalar(fld[:], fld[:], 190.0, None, ALU.min))
                V.tensor_scalar(inv[:], fld[:], -1.0, 254.0, ALU.mult, ALU.add)
                link(V.tensor_scalar(scl[:], fld[:], 23, None, ALU.logical_shift_left))
                link(V.tensor_scalar(inv[:], inv[:], 23, None, ALU.logical_shift_left))
                V.tensor_tensor(c2[:], inv[:].bitcast(f32)[:, 0:1], inv[:].bitcast(f32)[:, 1:2], ALU.mult)
                V.tensor_scalar(b1s[:], b1_sb[:], scl[:].bitcast(f32)[:, 0:1], None, ALU.mult).then_inc(s_scale, 1)

            par[0] = 0
            rows(0)
            for b in (-1, 0, 1, 2):
                step(b, b % 2)
            dve.wait_ge(s_w, 32)
            with dve.Fori(3, 6, 2) as b:
                step(b, 1, maxima=b - 3)
                step(b + 1, 0, maxima=b - 2)
            link(V.memset(small[:], 0.0))
            step(7, 1, hooks=(maxima_local, maxima_reduced, scales))
            dve.wait_ge(s_scale, 1)
            with dve.Fori(8, 13, 2) as b:
                step(b, 0, weights=b - 8)
                step(b + 1, 1, weights=b - 7)
            for b, e in ((14, 6), (15, 7), (16, None), (17, None)):
                step(b, b % 2, weights=e)

            def result(t, u):
                e = dve.value_load(expert_i[0:1, ds(t, 1)], min_val=0, max_val=E - 1)
                dve.wait_ge(m_down, t + 1)
                V.scalar_tensor_tensor(YT[:, ds(t, 1), :].rearrange("p a d -> p (a d)"), bank[4 + u][:, 0:D], c2[:],
                                       b2_sb[:, ds(e * D, D)], ALU.mult, ALU.add).then_inc(m_y, 1)

            def moe(t, u):
                if live(t, MOE_TILES):
                    dve.wait_ge(m_h, t + 1)
                    wait(dve, m_down, t - 1)
                    V.tensor_copy(Hs[:, u, 0, :], Hf[:, u, :]).then_inc(s_hi16, 1)
                    dve.wait_ge(s_hi16, t + 1)
                    V.tensor_tensor(Hs[:, u, 1, :], Hf[:, u, :], Hs[:, u, 0, :], ALU.subtract).then_inc(m_split, 1)
                if live(t - 1, MOE_TILES):
                    result(t - 1, 1 - u)
            for t in range(3):
                moe(t, t % 2)
            steps(dve, 3, MOE_TILES - 2, moe)
            moe(MOE_TILES - 1, 1)
            moe(MOE_TILES, 0)

            for g in range(4):
                dve.wait_ge(s_yb[g], 32)
                with dve.Fori(FC * g, FC * (g + 1)) as t:
                    for k in range(TOPK):
                        xt = X[:, ds(t, 1), :].rearrange("p a d -> p (a d)")
                        last = V.scalar_tensor_tensor(xt, YB[:, k, ds(t, 1), :].rearrange("p a d -> p (a d)"),
                                                      gates[:, k, ds(t, 1)], xt, ALU.mult, ALU.add).then_inc(s_comb, 1)
                        dve.wait_ge(s_comb, t * TOPK + k + 1)
                V.memset(small[:, 0, 0:1], 0.0).then_inc(s_fin, 1)

        @block.tensor
        def _(pe):
            mm = nc.tensor.matmul

            def three(ps, a_hi, a_lo, b_hi, b_lo, first=True, last=True):
                mm(ps, a_lo, b_hi, start=first, stop=False)
                mm(ps, a_hi, b_lo, start=False, stop=False)
                return mm(ps, a_hi, b_hi, start=False, stop=last)

            pe.wait_ge(s_early, 16 * 8)
            pe.wait_ge(s_const, 1)
            nc.tensor.transpose(bank[0][:, 0:P], Wq_sb[:], ident[:])
            nc.tensor.transpose(bank[0][:, P:2 * P], Wk_sb[:], ident[:]).then_inc(s_wt, 1)
            pe.wait_ge(s_rb, 1)
            pe.wait_ge(s_bqk, 1)
            mm(bank[3][:], BQK[:, 0:P], RB, start=True, stop=True)
            mm(bank[4][:], BQK[:, P:2 * P], RB, start=True, stop=True)
            pe.wait_ge(s_wtc, 1)
            mm(bank[1][:], WT[:, 0:P], RB, start=True, stop=True)
            mm(bank[2][:], WT[:, P:2 * P], RB, start=True, stop=True).then_inc(s_fold, 1)

            pe.wait_ge(s_bias, 1)
            pe.wait_ge(s_late, 16 * 5)

            def transposes(g, u):
                pe.wait_ge(s_pxn, g + 1)
                wait(pe, s_pxT, g - 1)
                for i in range(RT):
                    last = nc.tensor.transpose(bank[u][:, i * P:(i + 1) * P], XN[:, u, i, :], ident[:])
                last.then_inc(s_pT, 1)

            def router(g, u):
                if live(g + 1, RG):
                    transposes(g + 1, 1 - u)
                pe.wait_ge(s_pxT, g + 1)
                wait(pe, s_pL, g - 1)
                for i in range(RT):
                    last = mm(bank[2 + u][:, i * E:(i + 1) * E], XTR[:, u, i * P:(i + 1) * P], Wr_sb[:], start=True, stop=True)
                last.then_inc(s_plog, 1)
            transposes(0, 0)
            for g in range(3):
                router(g, g % 2)
            steps(pe, 3, RG - 2, router)
            router(RG - 1, 1)
            pe.wait_ge(s_oneh, 1)
            mm(bank[0][:], upper[:], ONEHOT16, start=True, stop=True)
            mm(bank[1][:], ones[:, 0:P], ONEHOT16, start=True, stop=True).then_inc(s_pfx, 1)

            par = [0]

            def parity(b):
                return b % 2 if isinstance(b, int) else par[0]

            def kproj(b, j, u):
                wait(pe, kf_ready, 2 * b - 1 + j)
                mm(psK[j][:], ones[:, 0:P], BIAS3[:, FEAT:2 * FEAT], start=True, stop=False)
                at = slice(j * P, (j + 1) * P)
                three(psK[j][:], xT_hi[:, u, at], xT_lo[:, u, at], WkR_hi[:], WkR_lo[:], first=False).then_inc(k_done, 1)

            def step(b, u, hooks=None):
                if live(b + 1):
                    pe.wait_ge(xn_ready, b + 2)
                    wait(pe, xlo_ready, b + 1)
                    wait(pe, xhi_ready, b + 1)
                    for j in range(NJ):
                        last = nc.tensor.transpose(psT[:, j * P:(j + 1) * P], XN[:, 1 - u, j, :], ident[:])
                    last.then_inc(xt_done, 1)
                if live(b - 1):
                    pe.wait_ge(v_ready, b)
                    pe.wait_ge(kf_ready, 2 * b)
                    for c in range(NC):
                        for j in range(NJ):
                            last = mm(psKV[:, c, :], KF[:, 1 - u, j, c * P:(c + 1) * P], VA[:, 1 - u, j, c, :],
                                      start=(j == 0), stop=(j == NJ - 1))
                    last.then_inc(kv_done, 1)
                if live(b):
                    pe.wait_ge(xhi_ready, b + 1)
                    pe.wait_ge(xlo_ready, b + 1)
                    kproj(b, 0, u)
                if live(b - 2):
                    pe.wait_ge(o_ready, b - 1)
                    wait(pe, base_ready, b - 2)
                    ov = O_sb[:].rearrange("p c w -> p (c w)")
                    for j in range(NJ):
                        last = nc.tensor.transpose(psOA[:, j * P:(j + 1) * P], ov[:, j * P:(j + 1) * P], ident[:])
                    last.then_inc(ot_done, 1)
                if hooks:
                    hooks[0]()
                if live(b):
                    kproj(b, 1, u)
                    wait(pe, bd_ready, b)
                    for j in range(NJ):
                        at, to = slice(j * P, (j + 1) * P), psV[:, j * D:(j + 1) * D]
                        mm(to, ones[:, 0:P], BIAS3[:, 2 * FEAT:2 * FEAT + D], start=True, stop=False)
                        last = three(to, xT_hi[:, u, at], xT_lo[:, u, at], Wv_hi[:], Wv_lo[:], first=False)
                    last.then_inc(v_done, 1)
                    for h in range(2):
                        wait(pe, qf_ready, 2 * b - 1 + h)
                        for i in range(2):
                            c = 2 * h + i
                            at, to = slice(c * P, (c + 1) * P), psQ[h][:, i * NJ * P:(i + 1) * NJ * P]
                            mm(to, BIAS3[:, at], ones[:], start=True, stop=False)
                            last = three(to, WqR_hi[:, at], WqR_lo[:, at], xT_hi[:, u, :], xT_lo[:, u, :], first=False)
                        last.then_inc(q_done, 1)
                        if hooks and h == 0:
                            hooks[1]()
                if live(b - 2):
                    pe.wait_ge(ot_ready, b - 1)
                    for j in range(NJ):
                        to = psOA[:, (NJ + j) * P:(NJ + j + 1) * P]
                        mm(to, ones[:, 0:P], BIAS3[:, 2 * FEAT + D:NBIAS], start=True, stop=False)
                        last = mm(to, OT_sb[:, j * P:(j + 1) * P], Wo_sb[:], start=False, stop=True)
                    last.then_inc(att_done, 1)
                if live(b - 1):
                    pe.wait_ge(bd_ready, b)
                    pe.wait_ge(qf_ready, 2 * b)
                    wait(pe, o_ready, b - 1)
                    if hooks:
                        pe.wait_ge(s_mread, 1)
                    for j in range(NJ):
                        for c in range(NC):
                            last = mm(psOut[:, j * NC + c, :], QF[:, 1 - u, c, j * P:(j + 1) * P], BD[:, c, :],
                                      start=True, stop=True)
                    last.then_inc(out_done, 1)

            def transpose_maxima():
                pe.wait_ge(s_mx, 1)
                nc.tensor.transpose(psO[0:3, 384:512], mx3[:], ident[:]).then_inc(s_mxT, 1)

            def broadcast_maxima():
                pe.wait_ge(s_m3, 1)
                mm(psO[:, 320:323], m3b[0:3, :], ident[0:3, 0:3], start=True, stop=True).then_inc(s_mb, 1)

            pe.wait_ge(s_slots, 1)
            for b in (-1, 0, 1, 2):
                step(b, b % 2)
            steps(pe, 3, 6, step)
            step(7, 1, hooks=(transpose_maxima, broadcast_maxima))
            steps(pe, 8, 13, step)
            for b in (14, 15, 16, 17):
                step(b, b % 2)

            words = SLOT_ROWS[:].bitcast(f16)

            def rows(t, u):
                wait(pe, m_xT, t - 1)
                for s in range(2):
                    last = nc.tensor.transpose(bank[u][:, s * P // 2:(s + 1) * P // 2].bitcast(f16),
                                               words[:, ds(t, 1), s * D:(s + 1) * D].rearrange("p a d -> p (a d)"), identh[:])
                last.then_inc(m_T, 1)

            def up(t, u):
                e = pe.value_load(expert_i[0:1, ds(t, 1)], min_val=0, max_val=E - 1)
                pe.wait_ge(m_xT, t + 1)
                wait(pe, m_h, t - 1)
                xh = XTS[:, u, 0:P // 2].bitcast(f16)
                xl = XTS[:, u, P // 2:P].bitcast(f16)
                for c in range(HCH):
                    to, at = bank[2 + u][:, c * P:(c + 1) * P], ds(e * HID + c * P, P)
                    mm(to, W1l[:, at], xh, start=True, stop=False)
                    mm(to, W1h[:, at], xl, start=False, stop=False)
                    last = mm(to, W1h[:, at], xh, start=False, stop=True)
                last.then_inc(m_up, 1)

            def down(t, u):
                e = pe.value_load(expert_i[0:1, ds(t, 1)], min_val=0, max_val=E - 1)
                pe.wait_ge(m_split, t + 1)
                wait(pe, m_y, t - 1)
                to = bank[4 + u][:, 0:D]
                for c in range(HCH):
                    at = ds(e * HID + c * P, P)
                    hh, hl = Hs[:, u, 0, c * P:(c + 1) * P], Hs[:, u, 1, c * P:(c + 1) * P]
                    mm(to, hl, W2h[:, at], start=(c == 0), stop=False)
                    mm(to, hh, W2l[:, at], start=False, stop=False)
                    last = mm(to, hh, W2h[:, at], start=False, stop=(c == HCH - 1))
                last.then_inc(m_down, 1)

            def moe(t, u):
                if live(t + 1, MOE_TILES):
                    rows(t + 1, 1 - u)
                if live(t, MOE_TILES):
                    up(t, u)
                if live(t - 1, MOE_TILES):
                    down(t - 1, 1 - u)

            pe.wait_ge(base_ready, NBATCH)
            pe.wait_ge(s_wsplit, E)
            pe.wait_ge(s_load[0], 16)
            rows(0, 0)
            for t in range(3):
                moe(t, t % 2)
            steps(pe, 3, FIRST_LOAD - 2, moe)
            pe.wait_ge(s_load[1], 16)
            steps(pe, FIRST_LOAD - 1, MOE_TILES - 2, moe)
            moe(MOE_TILES - 1, 1)
            moe(MOE_TILES, 0)


_INS = ["L0_attn_x", "L0_attn_Wq", "L0_attn_bq", "L0_attn_Wk", "L0_attn_bk", "L0_attn_Wv", "L0_attn_bv",
        "L0_attn_Wo", "L0_attn_bo", "L0_attn_random_matrix", "L0_ffn_Wr", "L0_ffn_br", "L0_ffn_W1",
        "L0_ffn_b1", "L0_ffn_W2", "L0_ffn_b2"]


def kernel(**inputs):
    import numpy as _np
    import concourse.bacc as _bacc
    from concourse import mybir as _mybir
    from concourse.bass_utils import run_bass_kernel_spmd as _run

    nc = _bacc.Bacc("TRN2", target_bir_lowering=False, num_devices=1)
    arrays, args = {}, []
    for name in _INS:
        a = _np.ascontiguousarray(inputs[name])
        arrays[f"in_{name}"] = a
        args.append(nc.dram_tensor(f"in_{name}", a.shape, _mybir.dt.from_np(a.dtype), kind="ExternalInput").ap())
    f32 = _mybir.dt.float32
    out = nc.dram_tensor("out_0", (NBATCH, NJ * P, D), f32, kind="ExternalOutput").ap()
    rows_dram = nc.dram_tensor("slot_rows", (SLOTS, ROWW), f32, kind="Internal").ap()
    y_dram = nc.dram_tensor("expert_results", (TOPK * T, D), f32, kind="Internal").ap()
    program(nc, *args, out, rows_dram, y_dram)
    r = _run(nc, [arrays], core_ids=[0])
    return r.results[0]["out_0"]
```

```python
import concourse.bass as bass
from concourse import mybir
from contextlib import ExitStack

P = 128
NBATCH = 16
NJ = 2
D = 128
NT = NBATCH * NJ
T = NT * P
HEADS, HD, M = 16, 8, 32
FEAT = HEADS * M
NC = FEAT // P
HC = P // M
KVW = HC * HD + HC
E, HID, TOPK = 8, 512, 2
HCH = HID // P
RT = 4
RG = NT // RT
SUB = 2
TS = SUB * P
TS_LOG2 = TS.bit_length() - 1
MOE_TILES = -(-(TOPK * T + E * (TS - 1)) // TS)
MOE_TILES += MOE_TILES % 2
SLOTS = MOE_TILES * TS
ROWW = D + 2
FIRST_LOAD = 8
PRE = 4
NO_ROW = TOPK * T
EPS = 1e-5
NORM_MIN = 1e-6 * 256.0
NEG = -3.0e38


def program(nc, x, wq, bq, wk, bk, wv, bv, wo, bo, rm, wr, br, w1, b1, w2, b2, out, rows_dram, y_dram):
    f32, f32r, f16, bf16 = mybir.dt.float32, mybir.dt.float32r, mybir.dt.float16, mybir.dt.bfloat16
    i32 = mybir.dt.int32
    ALU, ACT, AX = mybir.AluOpType, mybir.ActivationFunctionType, mybir.AxisListType
    ds = bass.ds

    with ExitStack() as ctx:
        def sb(name, shape, dt=f32):
            return ctx.enter_context(nc.sbuf_tensor(name, shape, dt))

        def sem(name):
            return ctx.enter_context(nc.semaphore(name))

        X = sb("X", [P, NT, D])
        SLOT_ROWS = sb("SLOT_ROWS", [P, MOE_TILES * SUB, ROWW])
        XS = SLOT_ROWS[:, 0:TOPK * NT, :].rearrange("p (k t) w -> p k t w", k=TOPK)
        YB = SLOT_ROWS[:, :, :].rearrange("p t w -> p (t w)")[:, 0:TOPK * NT * D].rearrange(
            "p (k t d) -> p k t d", k=TOPK, d=D)
        WRAW = sb("WRAW", [P, MOE_TILES * SUB * D])
        W1raw = WRAW[:, 0:E * HID].rearrange("p (e h) -> p e h", e=E)
        W2raw = WRAW[:, E * HID:2 * E * HID].rearrange("p (e h) -> p e h", e=E)
        YT = WRAW[:, :].rearrange("p (t d) -> p t d", d=D)
        W1h, W1l = sb("W1h", [P, E * HID], f16), sb("W1l", [P, E * HID], f16)
        W2h, W2l = sb("W2h", [P, E * HID], f16), sb("W2l", [P, E * HID], f16)
        PREFILL = sb("PREFILL", [P, PRE, ROWW])
        XN = sb("XN", [P, 2, RT, D])
        xT_hi, xT_lo = sb("xT_hi", [P, 2, NJ * P], f32r), sb("xT_lo", [P, 2, NJ * P], f32r)
        EK = sb("EK", [P, NJ, FEAT])
        KF = sb("KF", [P, 2, NJ, FEAT])
        EQ = sb("EQ", [P, NC, NJ * P])
        QF = sb("QF", [P, 2, NC, NJ * P])
        NBIAS = 2 * FEAT + 2 * D
        FOLD = WRAW[:, 0:2 * FEAT].rearrange("p (a n) -> p a n", a=2)
        B_REST = WRAW[:, 2 * FEAT:2 * FEAT + NBIAS]
        RB = EK[:, 0, :]
        WT = EK[:, 1, 0:2 * P]
        BQK = EK[:, 1, 2 * P:4 * P]
        XTR = EQ[:, :, :].rearrange("p c n -> p (c n)").rearrange("p (u n) -> p u n", u=2)
        KFflat = KF[:, :, :, :].rearrange("p a b c -> p (a b c)")
        QFflat = QF[:, :, :, :].rearrange("p a b c -> p (a b c)")
        B_REP = KFflat[:, 0:NBIAS]
        TMP = WRAW[:, 2 * E * HID:]
        ONEHOT = TMP[:, 0:512].rearrange("p (e k t) -> p e k t", e=E, k=TOPK)
        ONEHOT16 = TMP[:, 512:768].bitcast(bf16)
        CUM = TMP[:, 768:1280]
        SLOTM = TMP[:, 1280:1792]
        Hf = KFflat.rearrange("p (u n) -> p u n", u=2)
        Hs = QFflat.bitcast(f16).rearrange("p (u s n) -> p u s n", u=2, s=2)
        BIAS3 = sb("BIAS3", [P, NBIAS], bf16)
        pick3 = sb("pick3", [P, 2 * P], bf16)
        WqR_hi, WqR_lo = sb("WqR_hi", [P, FEAT], f32r), sb("WqR_lo", [P, FEAT], f32r)
        WkR_hi, WkR_lo = sb("WkR_hi", [P, FEAT], f32r), sb("WkR_lo", [P, FEAT], f32r)
        Wv_hi, Wv_lo = sb("Wv_hi", [P, D], f32r), sb("Wv_lo", [P, D], f32r)
        Wq_sb, Wk_sb, Wv_sb, Wo_sb = (sb(n, [P, D]) for n in ("Wq_sb", "Wk_sb", "Wv_sb", "Wo_sb"))
        Wr_sb, br_sb = sb("Wr_sb", [P, E]), sb("br_sb", [P, E])
        R_sb = sb("R_sb", [P, M])
        bqk_sb = sb("bqk_sb", [P, 2])
        b1_sb, b1s = sb("b1_sb", [P, E * HCH]), sb("b1s", [P, E * HCH])
        b2_sb = sb("b2_sb", [P, E * D])
        ident, identh = sb("ident", [P, P]), sb("identh", [P, P], f16)
        upper = sb("upper", [P, P], bf16)
        ones = sb("ones", [P, P], bf16)
        ones32 = sb("ones32", [P, 512])
        head_mask = sb("head_mask", [P, HEADS])
        bd_mask = sb("bd_mask", [P, KVW])
        rank8 = sb("rank8", [P, E])
        tile_no = sb("tile_no", [P, MOE_TILES])
        stats = sb("stats", [P, NT, 6])
        ln = sb("ln", [P, 8, NT])
        mean, rstd = ln[:, 0, :], ln[:, 1, :]
        L, L2, EQM = sb("L", [P, NT, E]), sb("L2", [P, NT, E]), sb("EQM", [P, NT, E])
        top = sb("top", [P, TOPK, NT])
        best = sb("best", [P, TOPK, NT])
        gates = sb("gates", [P, TOPK, NT])
        gtmp = sb("gtmp", [P, NT])
        small = sb("small", [P, 16, E])
        smalli = sb("smalli", [P, 4, E], i32)
        slot_f, slot_i = sb("slot_f", [P, TOPK * NT]), sb("slot_i", [P, TOPK * NT], i32)
        cmp = sb("cmp", [P, MOE_TILES, E])
        expert_f = sb("expert_f", [P, MOE_TILES])
        expert_i = sb("expert_i", [P, MOE_TILES // 2, 4], i32)
        VA = sb("VA", [P, 2, NJ, NC, KVW])
        BD = sb("BD", [P, NC, KVW])
        den = sb("den", [P, NJ * NC, HC])
        O_sb, OT_sb = sb("O_sb", [P, NJ * NC, HC * HD]), sb("OT_sb", [P, NJ * P])
        mx1, mx2, mx3 = sb("mx1", [P, 4]), sb("mx2", [P, 4]), sb("mx3", [P, 3])
        m3, m3b = sb("m3", [P, 1]), sb("m3b", [P, P])
        bound = sb("bound", [P, 2])
        fld, scl, inv = sb("fld", [P, 2], i32), sb("scl", [P, 2], i32), sb("inv", [P, 2], i32)
        c2 = sb("c2", [P, 1])
        neg1 = sb("neg1", [P, 1])
        XTS = sb("XTS", [P, 2, TS])

        bank = [ctx.enter_context(nc.psum_tensor(f"bank{i}", [P, 512], f32)) for i in range(8)]
        psT, psOA, psK, psQ, psVK, psO = bank[0], bank[1], bank[2:4], bank[4:6], bank[6], bank[7]
        psV = psVK[:, 160:160 + NJ * D]
        psKV = psVK[:, 0:NC * KVW].rearrange("p (c w) -> p c w", c=NC)
        psOut = psO[:, 0:NJ * NC * KVW].rearrange("p (c w) -> p c w", w=KVW)

        s_router_w, s_early, s_x, s_late, s_w = sem("router_weights"), sem("early_weights"), [sem(f"x_chunk{i}") for i in range(4)], sem("late_weights"), sem("expert_weights")
        s_const, s_pre, s_prefilled = sem("constants_made"), sem("prefill_made"), sem("slots_prefilled")
        s_wt, s_wtc, s_rb, s_bqk, s_fold, s_folded, s_vsplit, s_bias = (sem(n) for n in (
            "w_transposed", "w_transposed_copied", "rb_built", "bqk_repeated", "weights_folded",
            "weights_split_by_act", "weights_split_by_dve", "bias_parts_made"))
        s_var, s_sqrt = sem("variance_ready"), sem("sqrt_ready")
        s_pxn, s_phi, s_plo, s_pT, s_pxT, s_plog, s_pL = (sem(n) for n in (
            "router_rows_normalised", "router_hi_written", "router_lo_written", "router_transposed",
            "router_transposed_copied", "router_logits_done", "router_logits_read"))
        s_dup, s_ids = sem("rows_duplicated"), sem("row_numbers_written")
        s_gates = sem("gates_written")
        s_gd, s_gexp, s_oneh, s_pfx, s_slots = (sem(n) for n in (
            "gate_difference", "gate_exp", "onehot_ready", "prefixes_done", "slots_ready"))
        s_bpart, s_brest = sem("bias_part"), sem("bias_rest")
        s_scat = sem("rows_scattered")
        s_load = [sem("slots_loaded_first"), sem("slots_loaded_rest")]
        s_dve, s_pool, s_act = sem("dve_step"), sem("pool_step"), sem("act_step")
        (xn_ready, xt_done, xhi_ready, xlo_ready, k_done, v_done, q_done, ek_ready, kf_ready, eq_ready,
         qf_ready, v_ready, kv_done, bd_ready, out_done, o_ready, ot_done, ot_ready, att_done,
         base_ready) = (sem(n) for n in (
             "xn_ready", "xt_done", "xhi_ready", "xlo_ready", "k_done", "v_done", "q_done", "ek_ready",
             "kf_ready", "eq_ready", "qf_ready", "v_ready", "kv_done", "bd_ready", "out_done", "o_ready",
             "ot_done", "ot_ready", "att_done", "base_ready"))
        s_mx, s_mxT, s_m3, s_mb, s_scale, s_wsplit, s_whi = (sem(n) for n in (
            "weight_maxima", "maxima_transposed", "maxima_reduced", "maxima_broadcast", "scales_ready",
            "expert_weights_lo", "expert_weights_hi"))
        m_yraw = sem("y_ungated")
        (m_T, m_xT, m_up, m_h, m_split, m_down, m_y) = (sem(n) for n in (
            "slot_rows_transposed", "slot_rows_copied", "up_done", "hidden_ready", "hidden_split",
            "down_done", "y_ready"))
        s_mread = sem("maxima_read")
        s_ysc = sem("y_scattered")
        s_yb = [sem(f"y_back{i}") for i in range(4)]
        s_fin, s_comb, s_norm, s_hi16 = sem("chunk_combined"), sem("tile_combined"), sem("norm_step"), sem("hidden_hi")
        s_out = sem("out_written")

        block = ctx.enter_context(nc.Block())
        FC = NT // 4

        def wait(eng, semaphore, value):
            if not isinstance(value, int) or value > 0:
                eng.wait_ge(semaphore, value)

        def spread(ap, dim, n):
            return ap.broadcast_to([n if i == dim else size for i, size in enumerate(ap.shape)])

        def live(b, n=NBATCH):
            return not isinstance(b, int) or 0 <= b < n

        def steps(eng, first, last, body):
            with eng.Fori(first, last, 2) as b:
                body(b, first % 2)
                body(b + 1, (first + 1) % 2)

        def experts(engine, g):
            return nc.values_load_multi_w_load_instructions(
                expert_i[0:1, ds(g, 1), :].rearrange("p g i -> p (g i)"), engines=[engine], min_val=0, max_val=E - 1,
                skip_runtime_bounds_check_because="the program clamps them to E - 1")[1]

        def up_bank(u, c):
            return bank[2 + 2 * u + c // 2][:, (c % 2) * TS:(c % 2 + 1) * TS]

        def x_view(dram):
            return dram.rearrange("b (p j) d -> p b j d", j=NJ)

        @block.sync
        def _(sp):
            for g in range(4):
                sp.dma_start(X[:, FC * g:FC * (g + 1), :].rearrange("p (b j) d -> p b j d", j=NJ),
                             x_view(x)[:, g * FC // NJ:(g + 1) * FC // NJ]).then_inc(s_x[g], 16)
            sp.wait_ge(s_pre, 1)
            sp.wait_ge(s_x[3], 16)
            pre = rows_dram.rearrange("(g p t) w -> g p t w", p=P, t=PRE)
            for g in range(SLOTS // (P * PRE)):
                sp.dma_start(pre[g], PREFILL[:]).then_inc(s_prefilled, 16)
            sp.wait_ge(s_bias, 1)
            sp.dma_start(W1raw, w1.rearrange("e d h -> d e h")).then_inc(s_w, 16)
            sp.dma_start(W2raw.rearrange("p e (c o) -> p e c o", c=HCH),
                         w2.rearrange("e (p c) o -> p e c o", c=HCH)).then_inc(s_w, 16)
            sp.wait_ge(s_scat, 16 * TOPK * NT)
            slots = rows_dram.rearrange("(t p) w -> p t w", p=P)
            sp.dma_start(SLOT_ROWS[:, 0:FIRST_LOAD * SUB, :], slots[:, 0:FIRST_LOAD * SUB]).then_inc(s_load[0], 16)
            sp.dma_start(SLOT_ROWS[:, FIRST_LOAD * SUB:, :], slots[:, FIRST_LOAD * SUB:]).then_inc(s_load[1], 16)
            sp.wait_ge(s_ysc, 16 * MOE_TILES * SUB)
            yv = y_dram.rearrange("(k p t) d -> p k t d", k=TOPK, p=P)
            for g in range(4):
                for k in range(TOPK):
                    sp.dma_start(YB[:, k, FC * g:FC * (g + 1), :], yv[:, k, FC * g:FC * (g + 1)]).then_inc(s_yb[g], 16)
            for g in range(4):
                sp.wait_ge(s_fin, g + 1)
                sp.dma_start(x_view(out)[:, g * FC // NJ:(g + 1) * FC // NJ],
                             X[:, FC * g:FC * (g + 1), :].rearrange("p (b j) d -> p b j d", j=NJ)).then_inc(s_out, 16)
            sp.wait_ge(s_out, 64)

        @block.gpsimd
        def _(pool):
            count = [0]

            def link(ins):
                count[0] += 1
                ins.then_inc(s_pool, 1)
                pool.wait_ge(s_pool, count[0])

            def keep(t, op, base, pattern, mult):
                link(nc.gpsimd.affine_select(out=t, in_=t, compare_op=op, fill=0.0, base=base,
                                             pattern=pattern, channel_multiplier=mult))

            for t in (ident, upper, ones, pick3, ones32, bd_mask, head_mask, VA):
                nc.gpsimd.memset(t[:], 1.0)
            link(nc.gpsimd.memset(PREFILL[:], 0.0))
            nc.gpsimd.memset(PREFILL[:].bitcast(i32)[:, :, D], NO_ROW).then_inc(s_pre, 1)
            keep(ident[:], ALU.is_equal, 0, [[1, P]], -1)
            link(nc.gpsimd.tensor_copy(identh[:], ident[:]))
            keep(head_mask[:], ALU.is_ge, 0, [[-HD, HEADS]], 1)
            keep(head_mask[:], ALU.is_ge, HD - 1, [[HD, HEADS]], -1)
            for v, inner in ((bd_mask[:, 0:HC * HD], [[0, HD]]), (bd_mask[:, HC * HD:KVW], [])):
                keep(v, ALU.is_ge, 0, [[-M, HC]] + inner, 1)
                keep(v, ALU.is_ge, M - 1, [[M, HC]] + inner, -1)
            keep(upper[:], ALU.is_gt, 0, [[1, P]], -1)
            for row in (0, 64, 96):
                V3 = pick3[row:row + 32, :]
                keep(V3, ALU.is_equal, 0, [[0, 2 * P]], 1)
            keep(pick3[32:64, :], ALU.is_gt, 0, [[0, 2 * P]], -1)
            nc.gpsimd.iota(rank8[:], pattern=[[-1, E]], base=E, channel_multiplier=0,
                           allow_small_or_imprecise_dtypes=True)
            link(nc.gpsimd.iota(tile_no[:], pattern=[[1, MOE_TILES]], base=0, channel_multiplier=0,
                                allow_small_or_imprecise_dtypes=True))
            nc.gpsimd.iota(XS.bitcast(i32)[:, :, :, D], pattern=[[T, TOPK], [1, NT]], base=0,
                           channel_multiplier=NT).then_inc(s_const, 1)

            G = nc.gpsimd
            pool.wait_ge(s_early, 16 * 8)
            G.tensor_copy(BQK.rearrange("p (a n) -> p a n", a=2), spread(bqk_sb[:].unsqueeze(2), 2, P))
            G.tensor_tensor(RB.rearrange("p (h m) -> p h m", h=HEADS), spread(R_sb[:].unsqueeze(1), 1, HEADS),
                            spread(head_mask[:].unsqueeze(2), 2, M), ALU.mult).then_inc(s_rb, 1)
            pool.wait_ge(s_folded, 1)
            G.tensor_tensor(WqR_lo[:], FOLD[:, 0, :], WqR_hi[:].bitcast(f32), ALU.subtract)
            G.tensor_tensor(WkR_lo[:], FOLD[:, 1, :], WkR_hi[:].bitcast(f32), ALU.subtract)
            G.tensor_tensor(Wv_lo[:], Wv_sb[:], Wv_hi[:].bitcast(f32), ALU.subtract)
            for n in range(2):
                pool.wait_ge(s_bpart, n + 1)
                G.tensor_tensor(B_REST, B_REST if n else B_REP, BIAS3[:], ALU.subtract).then_inc(s_brest, 1)
                pool.wait_ge(s_brest, n + 1)
            pool.wait_ge(s_dup, RG)
            pool.wait_ge(s_gates, 1)
            pool.wait_ge(s_slots, 1)
            pool.wait_ge(s_prefilled, 16 * (SLOTS // (P * PRE)))
            for c in range(TOPK * NT):
                nc.gpsimd.indirect_dma_start(
                    rows_dram, bass.IndirectOffsetOnAxis(ap=slot_i[:, c:c + 1], axis=0),
                    XS[:, c // NT, c % NT, :], None).then_inc(s_scat, 16)
            ids = SLOT_ROWS[:].bitcast(i32)
            pool.wait_ge(s_load[0], 16)
            for t in range(MOE_TILES * SUB):
                if t == FIRST_LOAD * SUB:
                    pool.wait_ge(s_load[1], 16)
                if t % SUB == 0:
                    pool.wait_ge(m_y, t // SUB + 1)
                nc.gpsimd.indirect_dma_start(
                    y_dram, bass.IndirectOffsetOnAxis(ap=ids[:, t, D:D + 1], axis=0), YT[:, t, :], None,
                    bounds_check=NO_ROW - 1, oob_is_err=False).then_inc(s_ysc, 16)

        @block.scalar
        def _(act):
            for dst, src in ((Wr_sb[:], wr), (br_sb[:], br.partition_broadcast(P))):
                act.dma_start(dst, src).then_inc(s_router_w, 16)
            for dst, src in ((Wq_sb[:], wq), (Wk_sb[:], wk), (bqk_sb[:, 0:1], bq.unsqueeze(1)),
                             (bqk_sb[:, 1:2], bk.unsqueeze(1)), (Wv_sb[:], wv)):
                act.dma_start(dst, src).then_inc(s_early, 16)
            act.dma_start(R_sb[:], bass.AP(rm.tensor, 0, [[0, P // HD], [M, HD], [1, M]])).then_inc(s_early, 16)
            act.dma_start(B_REP[:, 2 * FEAT:2 * FEAT + D], bv.partition_broadcast(P)).then_inc(s_early, 16)
            act.dma_start(B_REP[:, 2 * FEAT + D:NBIAS], bo.partition_broadcast(P)).then_inc(s_early, 16)
            act.dma_start(Wo_sb[:], wo).then_inc(s_late, 16)
            act.dma_start(b1_sb[:].rearrange("p (e c) -> p e c", e=E), b1.rearrange("e (p c) -> p e c", c=HCH)).then_inc(s_late, 16)
            act.dma_start(b2_sb[:], b2.rearrange("e o -> (e o)").partition_broadcast(P)).then_inc(s_late, 16)

            act.wait_ge(s_var, 1)
            nc.scalar.activation(ln[:, 3, :], ln[:, 2, :], ACT.Sqrt).then_inc(s_sqrt, 1)

            def router(g, u):
                act.wait_ge(s_pxn, g + 1)
                nc.scalar.copy(XS[:, 0, ds(g * RT, RT), 0:D // 2].bitcast(f16), XN[:, u]).then_inc(s_phi, 1)
                act.wait_ge(s_pT, g + 1)
                wait(act, s_plog, g - 1)
                nc.scalar.copy(XTR[:, u, :], bank[u][:]).then_inc(s_pxT, 1)

            def dup(g):
                act.wait_ge(s_plo, g + 1)
                nc.scalar.copy(XS[:, 1, g * RT:(g + 1) * RT, 0:D], XS[:, 0, g * RT:(g + 1) * RT, 0:D]).then_inc(s_dup, 1)

            def setup():
                act.wait_ge(s_wt, 1)
                nc.scalar.copy(WT, bank[3][:, 0:2 * P]).then_inc(s_wtc, 1)
                act.wait_ge(s_fold, 1)
                nc.scalar.copy(WqR_hi[:], bank[4][:])
                nc.scalar.copy(WkR_hi[:], bank[5][:])
                nc.scalar.copy(FOLD[:, 0, :], bank[4][:])
                nc.scalar.copy(FOLD[:, 1, :], bank[5][:])
                nc.scalar.activation(B_REP[:, 0:FEAT], bank[6][:], ACT.Identity, bias=ones32[:, 0:1])
                nc.scalar.activation(B_REP[:, FEAT:2 * FEAT], bank[7][:], ACT.Identity, bias=ones32[:, 0:1])
                act.wait_ge(s_early, 16 * 8)
                nc.scalar.copy(Wv_hi[:], Wv_sb[:]).then_inc(s_folded, 1)

            def bias_part(n):
                if n:
                    act.wait_ge(s_brest, n)
                rows = slice((0, 64, 96)[n], P)
                nc.scalar.copy(BIAS3[rows, :], (B_REST if n else B_REP)[rows, :]).then_inc(s_bpart if n < 2 else s_bias, 1)

            for g in range(RG):
                router(g, g % 2)
                if g:
                    dup(g - 1)
                if g == 1:
                    setup()
                    act.wait_ge(s_folded, 1)
                if g in (1, 4, 7):
                    bias_part(g // 3)
            dup(RG - 1)

            def hi_part(b):
                if not live(b):
                    return
                u = parity(b)
                act.wait_ge(xt_done, b + 1)
                wait(act, q_done, 2 * b - 2)
                nc.scalar.copy(xT_hi[:, u, :], psT[:, 0:NJ * P]).then_inc(xhi_ready, 1)

            par = [0]

            def parity(b):
                return b % 2 if isinstance(b, int) else par[0]

            def step(b, u, weights=None):
                par[0] = 1 - u
                hi_part(b + 1)
                par[0] = u
                if live(b):
                    for j in range(NJ):
                        act.wait_ge(k_done, 2 * b + j + 1)
                        wait(act, kf_ready, 2 * b - 1 + j)
                        nc.scalar.activation(EK[:, j, :], psK[j][:], ACT.Exp, bias=neg1[:, 0:1]).then_inc(ek_ready, 1)
                if live(b - 2):
                    act.wait_ge(ot_done, b - 1)
                    wait(act, att_done, b - 2)
                    nc.scalar.copy(OT_sb[:], psOA[:, 0:NJ * P]).then_inc(ot_ready, 1)
                if live(b):
                    for h in range(2):
                        act.wait_ge(q_done, 2 * b + h + 1)
                        wait(act, qf_ready, 2 * b - 1 + h)
                        nc.scalar.activation(EQ[:, 2 * h:2 * h + 2, :].rearrange("p c n -> p (c n)"), psQ[h][:],
                                             ACT.Exp, bias=neg1[:, 0:1]).then_inc(eq_ready, 1)
                        if h == 0:
                            act.wait_ge(v_done, b + 1)
                            wait(act, kv_done, b - 1)
                            nc.scalar.copy(VA[:, u, :, :, 0:HC * HD],
                                           psV.rearrange("p (j c w) -> p j c w", j=NJ, c=NC)).then_inc(v_ready, 1)
                if weights is not None:
                    for raw, hi, s in ((W1raw[:, ds(weights, 1), :].rearrange("p e (a c) -> p (e c) a", c=HCH), W1h, 0),
                                       (W2raw[:, ds(weights, 1), :].rearrange("p e (c a) -> p (e c) a", c=HCH), W2h, 1)):
                        last = nc.scalar.activation(hi[:, ds(weights * HID, HID)].rearrange("p (c a) -> p c a", c=HCH), raw,
                                                    ACT.Copy, scale=scl[:].bitcast(f32)[:, s:s + 1])
                    last.then_inc(s_whi, 1)

            act.wait_ge(s_const, 1)
            step(-1, 1)
            act.wait_ge(s_gd, 1)
            nc.scalar.activation(gtmp[:], gtmp[:], ACT.Exp).then_inc(s_gexp, 1)
            for b in (0, 1, 2):
                step(b, b % 2)
            steps(act, 3, 6, step)
            step(7, 1)
            act.wait_ge(s_scale, 1)
            with act.Fori(8, 13, 2) as b:
                step(b, 0, b - 8)
                step(b + 1, 1, b - 7)
            for b, e in ((14, 6), (15, 7), (16, None), (17, None)):
                step(b, b % 2, e)

            def copy_rows(t, u):
                act.wait_ge(m_T, t + 1)
                wait(act, m_up, t - 1)
                nc.scalar.copy(XTS[:, u, :], bank[u][:, 0:TS]).then_inc(m_xT, 1)

            def moe(t, u, e):
                if live(t + 1, MOE_TILES):
                    copy_rows(t + 1, 1 - u)
                act.wait_ge(m_up, t + 1)
                wait(act, m_split, t - 1)
                for c in range(HCH):
                    last = nc.scalar.activation(Hf[:, u, c * TS:(c + 1) * TS], up_bank(u, c), ACT.Relu,
                                                bias=b1s[:, ds(e * HCH + c, 1)])
                last.then_inc(m_h, 1)
            copy_rows(0, 0)
            e = experts(mybir.EngineType.Activation, 0)
            for t in range(3):
                moe(t, t % 2, e[t])
            with act.Fori(1, MOE_TILES // 2 - 1) as g:
                e = experts(mybir.EngineType.Activation, g)
                moe(2 * g + 1, 1, e[1])
                moe(2 * g + 2, 0, e[2])
            e = experts(mybir.EngineType.Activation, MOE_TILES // 2 - 1)
            moe(MOE_TILES - 1, 1, e[1])

        @block.vector
        def _(dve):
            count = [0]

            def link(ins):
                count[0] += 1
                ins.then_inc(s_dve, 1)
                dve.wait_ge(s_dve, count[0])

            V = nc.vector
            nc.vector.memset(neg1[:], -1.0)
            for g in range(4):
                dve.wait_ge(s_x[g], 16)
                for t in range(FC * g, FC * (g + 1)):
                    V.bn_stats(stats[:, t, :], X[:, t, :])
            link(V.memset(small[:], 0.0))
            me, se, mo, so = stats[:, :, 1], stats[:, :, 2], stats[:, :, 4], stats[:, :, 5]
            a, v, y, z = ln[:, 4, :], ln[:, 2, :], ln[:, 5, :], ln[:, 6, :]
            V.tensor_tensor(a, me, mo, ALU.add)
            V.tensor_tensor(y, me, mo, ALU.subtract)
            link(V.tensor_tensor(v, se, so, ALU.add))
            V.tensor_scalar(mean, a, 0.5, None, ALU.mult)
            link(V.scalar_tensor_tensor(y, y, 0.25, y, ALU.mult, ALU.mult))
            link(V.scalar_tensor_tensor(v, v, 1.0 / D, y, ALU.mult, ALU.add))
            V.tensor_scalar(v, v, EPS, None, ALU.add).then_inc(s_var, 1)
            dve.wait_ge(s_sqrt, 1)
            link(V.reciprocal(y, ln[:, 3, :]))
            link(V.tensor_tensor(z, y, y, ALU.mult))
            link(V.tensor_tensor(z, z, v, ALU.mult))
            link(V.tensor_scalar(z, z, -0.5, 1.5, ALU.mult, ALU.add))
            link(V.tensor_tensor(rstd, y, z, ALU.mult))

            def normalise(tile, dst):
                return V.tensor_scalar(dst, X[:, ds(tile, 1), :].rearrange("p a d -> p (a d)"),
                                       mean[:, ds(tile, 1)], rstd[:, ds(tile, 1)], ALU.subtract, ALU.mult)

            def logits(g, u):
                dve.wait_ge(s_plog, g + 1)
                V.tensor_tensor(L[:, ds(g * RT, RT), :], bank[2 + u][:, 0:RT * E].rearrange("p (t e) -> p t e", e=E),
                                spread(br_sb[:].unsqueeze(1), 1, RT), ALU.add).then_inc(s_pL, 1)

            def group_rows(g, u):
                wait(dve, s_pT, g - 1)
                wait(dve, s_phi, g - 1)
                wait(dve, s_plo, g - 1)
                for i in range(RT):
                    last = normalise(g * RT + i, XN[:, u, i, :])
                last.then_inc(s_pxn, 1)

            def router(g, u):
                if live(g + 1, RG):
                    group_rows(g + 1, 1 - u)
                dve.wait_ge(s_phi, g + 1)
                dve.wait_ge(s_pxn, g + 1)
                V.tensor_tensor(XS[:, 0, ds(g * RT, RT), D // 2:D].bitcast(f16), XN[:, u],
                                XS[:, 0, ds(g * RT, RT), 0:D // 2].bitcast(f16), ALU.subtract).then_inc(s_plo, 1)
                if live(g - 1):
                    logits(g - 1, 1 - u)
            dve.wait_ge(s_router_w, 32)
            dve.wait_ge(s_const, 1)
            group_rows(0, 0)
            for g in range(RG):
                router(g, g % 2)
            logits(RG - 1, (RG - 1) % 2)
            dve.wait_ge(s_pL, RG)

            par = [0]

            def parity(b):
                return b % 2 if isinstance(b, int) else par[0]

            def rows(b):
                if live(b):
                    wait(dve, xt_done, b - 1)
                    for j in range(NJ):
                        last = normalise(b * NJ + j, XN[:, parity(b), j, :])
                    last.then_inc(xn_ready, 1)

            def lo_part(b):
                if live(b):
                    u = parity(b)
                    dve.wait_ge(xhi_ready, b + 1)
                    V.tensor_tensor(xT_lo[:, u, :], psT[:, 0:NJ * P], xT_hi[:, u, :].bitcast(f32),
                                    ALU.subtract).then_inc(xlo_ready, 1)

            def masked_kv(b):
                if live(b):
                    dve.wait_ge(kv_done, b + 1)
                    wait(dve, out_done, b)
                    V.tensor_tensor(BD[:], psKV, spread(bd_mask[:].unsqueeze(1), 1, NC), ALU.mult).then_inc(bd_ready, 1)

            def step(b, u, maxima=None, weights=None, hooks=None):
                par[0] = u
                rows(b + 2)
                par[0] = 1 - u
                lo_part(b + 1)
                par[0] = u
                if hooks:
                    hooks[0]()
                if live(b):
                    for j in range(NJ):
                        dve.wait_ge(ek_ready, 2 * b + j + 1)
                        wait(dve, kv_done, b - 1)
                        V.scalar_tensor_tensor(KF[:, u, j, :], EK[:, j, :], 1.0, psK[j][:], ALU.min, ALU.max).then_inc(kf_ready, 1)
                        if j == 0:
                            masked_kv(b - 1)
                        if hooks and j == 1:
                            hooks[1]()
                    for h in range(2):
                        dve.wait_ge(eq_ready, 2 * b + h + 1)
                        wait(dve, out_done, b - 1)
                        V.scalar_tensor_tensor(QF[:, u, 2 * h:2 * h + 2, :].rearrange("p c n -> p (c n)"),
                                               EQ[:, 2 * h:2 * h + 2, :].rearrange("p c n -> p (c n)"), 1.0,
                                               psQ[h][:], ALU.min, ALU.max).then_inc(qf_ready, 1)
                        if hooks and h == 0:
                            hooks[2]()
                else:
                    masked_kv(b - 1)
                if live(b - 1):
                    dve.wait_ge(out_done, b)
                    link2(V.tensor_scalar(den[:], psOut[:, :, HC * HD:KVW], NORM_MIN, None, ALU.max), b)
                    link2(V.reciprocal(den[:], den[:]), b)
                    wait(dve, ot_done, b - 1)
                    V.tensor_tensor(O_sb[:].rearrange("p c (h d) -> p c h d", h=HC),
                                    psOut[:, :, 0:HC * HD].rearrange("p c (h d) -> p c h d", h=HC),
                                    spread(den[:].unsqueeze(3), 3, HD), ALU.mult).then_inc(o_ready, 1)
                if live(b - 2):
                    dve.wait_ge(att_done, b - 1)
                    xb = X[:, ds((b - 2) * NJ, NJ), :]
                    V.tensor_tensor(xb, psOA[:, NJ * P:2 * NJ * P].rearrange("p (j d) -> p j d", j=NJ), xb,
                                    ALU.add).then_inc(base_ready, 1)
                if maxima is not None:
                    for raw, m in ((W1raw, mx1), (W2raw, mx2)):
                        V.tensor_reduce(m[:, ds(maxima, 1)], raw[:, ds(maxima * 2, 2), :].rearrange("p e h -> p (e h)"), AX.X, ALU.max,
                                        apply_absolute_value=True)
                if weights is not None:
                    dve.wait_ge(s_whi, weights + 1)
                    for raw, hi, lo, s in (
                            (W1raw[:, ds(weights, 1), :].rearrange("p e (a c) -> p (e c) a", c=HCH), W1h, W1l, 0),
                            (W2raw[:, ds(weights, 1), :].rearrange("p e (c a) -> p (e c) a", c=HCH), W2h, W2l, 1)):
                        at = ds(weights * HID, HID)
                        last = V.scalar_tensor_tensor(lo[:, at].rearrange("p (c a) -> p c a", c=HCH), raw,
                                                      scl[:].bitcast(f32)[:, s:s + 1],
                                                      hi[:, at].rearrange("p (c a) -> p c a", c=HCH), ALU.mult, ALU.subtract)
                    last.then_inc(s_wsplit, 1)

            def link2(ins, b):
                norm_half[0] ^= 1
                ins.then_inc(s_norm, 1)
                dve.wait_ge(s_norm, 2 * b - norm_half[0])
            norm_half = [0]

            def maxima_local():
                V.tensor_reduce(mx3[:, 0:1], mx1[:], AX.X, ALU.max)
                V.tensor_reduce(mx3[:, 1:2], mx2[:], AX.X, ALU.max)
                V.tensor_reduce(mx3[:, 2:3], b1_sb[:], AX.X, ALU.max, apply_absolute_value=True).then_inc(s_mx, 1)

            def maxima_reduced():
                dve.wait_ge(s_mxT, 1)
                link(V.tensor_reduce(m3[0:3, :], psO[0:3, 384:512], AX.X, ALU.max))
                V.tensor_copy(m3b[0:3, :], spread(m3[0:3, 0:1], 1, P)).then_inc(s_m3, 1)

            def scales():
                dve.wait_ge(s_mb, 1)
                V.tensor_copy(bound[:, 1:2], psO[:, 321:322])
                link(V.tensor_copy(c2[:], psO[:, 322:323]))
                V.scalar_tensor_tensor(bound[:, 0:1], psO[:, 320:321], float(D), c2[:], ALU.mult, ALU.add).then_inc(s_mread, 1)
                dve.wait_ge(s_mread, 1)
                link(V.tensor_scalar(fld[:], bound[:].bitcast(i32), 23, None, ALU.logical_shift_right))
                link(V.tensor_scalar(fld[:], fld[:], -1.0, 268.0, ALU.mult, ALU.add))
                link(V.tensor_scalar(fld[:], fld[:], 190.0, None, ALU.min))
                V.tensor_scalar(inv[:], fld[:], -1.0, 254.0, ALU.mult, ALU.add)
                link(V.tensor_scalar(scl[:], fld[:], 23, None, ALU.logical_shift_left))
                link(V.tensor_scalar(inv[:], inv[:], 23, None, ALU.logical_shift_left))
                V.tensor_tensor(c2[:], inv[:].bitcast(f32)[:, 0:1], inv[:].bitcast(f32)[:, 1:2], ALU.mult)
                V.tensor_scalar(b1s[:], b1_sb[:], scl[:].bitcast(f32)[:, 0:1], None, ALU.mult).then_inc(s_scale, 1)

            def choose():
                def bc_e(t):
                    return spread(t.unsqueeze(2), 2, E)
                rank_b = spread(rank8[:].unsqueeze(1), 1, NT)
                src = L
                for k in range(TOPK):
                    link(V.tensor_reduce(top[:, k, :], src[:], AX.X, ALU.max))
                    link(V.tensor_tensor(EQM[:], src[:], bc_e(top[:, k, :]), ALU.is_equal))
                    link(V.tensor_tensor(EQM[:], EQM[:], rank_b, ALU.mult))
                    link(V.tensor_reduce(best[:, k, :], EQM[:], AX.X, ALU.max))
                    oh = ONEHOT[:, :, k, :].rearrange("p e t -> p t e")
                    link(V.tensor_tensor(oh, bc_e(best[:, k, :]), rank_b, ALU.is_equal))
                    if k == 0:
                        link(V.scalar_tensor_tensor(L2[:], oh, NEG, L[:], ALU.mult, ALU.add))
                        src = L2
                ohf = ONEHOT.rearrange("p e k t -> p (e k t)")
                V.tensor_copy(ONEHOT16, ohf).then_inc(s_oneh, 1)
                V.tensor_tensor(gtmp[:], top[:, 1, :], top[:, 0, :], ALU.subtract).then_inc(s_gd, 1)

            def rank():
                dve.wait_ge(s_pfx, 1)
                TOT, PFX = bank[7], bank[1]
                link(V.tensor_tensor_scan(CUM, ones32[:], TOT[:], 0.0, ALU.mult, ALU.add))
                cume = CUM.rearrange("p (e n) -> p e n", e=E)
                cinc, n, ntile, tinc, tf, cex, delta = (small[:, i, :] for i in range(1, 8))
                V.tensor_copy(cinc, cume[:, :, TOPK * NT - 1])
                link(V.memset(cex[:, 0:1], 0.0))
                link(V.tensor_copy(cex[:, 1:E], cinc[:, 0:E - 1]))
                link(V.tensor_tensor(n, cinc, cex, ALU.subtract))
                link(V.tensor_scalar(smalli[:, 0, :], n, float(TS - 1), None, ALU.add))
                link(V.tensor_scalar(smalli[:, 1, :], smalli[:, 0, :], TS_LOG2, None, ALU.logical_shift_right))
                link(V.tensor_copy(ntile, smalli[:, 1, :]))
                link(V.tensor_tensor_scan(tinc, ones32[:, 0:E], ntile, 0.0, ALU.mult, ALU.add))
                link(V.tensor_tensor(tf, tinc, ntile, ALU.subtract))
                link(V.scalar_tensor_tensor(delta, tf, float(TS), cex, ALU.mult, ALU.subtract))
                link(V.tensor_tensor(SLOTM, CUM, TOT[:], ALU.subtract))
                link(V.tensor_tensor(SLOTM, SLOTM, PFX[:], ALU.add))
                sl = SLOTM.rearrange("p (e n) -> p e n", e=E)
                link(V.tensor_tensor(sl, sl, spread(delta.unsqueeze(2), 2, TOPK * NT), ALU.add))
                link(V.tensor_tensor(SLOTM, SLOTM, ONEHOT.rearrange("p e k t -> p (e k t)"), ALU.mult))
                link(V.tensor_reduce(slot_f[:], SLOTM.rearrange("p (e n) -> p n e", e=E), AX.X, ALU.add))
                V.tensor_copy(slot_i[:], slot_f[:]).then_inc(s_slots, 1)
                return tinc

            def weigh():
                dve.wait_ge(s_gexp, 1)
                link(V.tensor_scalar(best[:, 0, :], gtmp[:], 1.0, None, ALU.add))
                link(V.reciprocal(gates[:, 0, :], best[:, 0, :]))
                link(V.tensor_tensor(gates[:, 1, :], gates[:, 0, :], gtmp[:], ALU.mult))
                V.tensor_copy(XS[:, :, :, D + 1], gates[:]).then_inc(s_gates, 1)

            def tile_experts(tinc):
                link(V.tensor_tensor(cmp[:], spread(tile_no[:].unsqueeze(2), 2, E),
                                     spread(tinc.unsqueeze(1), 1, MOE_TILES), ALU.is_ge))
                link(V.tensor_reduce(expert_f[:], cmp[:], AX.X, ALU.add))
                pairs = expert_f[:].rearrange("p (g i) -> p g i", i=2)
                G = MOE_TILES // 2
                V.tensor_scalar(expert_i[:, :, 0:2], pairs, float(E - 1), None, ALU.min)
                V.tensor_scalar(expert_i[:, 0:G - 1, 2:4], pairs[:, 1:G, :], float(E - 1), None, ALU.min)
                link(V.tensor_scalar(expert_i[:, G - 1:G, 2:4], pairs[:, G - 1:G, :], float(E - 1), None, ALU.min))

            par[0] = 0
            rows(0)
            step(-1, 1)
            choose()
            weigh()
            step(0, 0)
            ends = rank()
            step(1, 1)
            tile_experts(ends)
            step(2, 0)
            dve.wait_ge(s_w, 32)
            with dve.Fori(3, 6, 2) as b:
                step(b, 1, maxima=b - 3)
                step(b + 1, 0, maxima=b - 2)
            link(V.memset(small[:], 0.0))
            step(7, 1, hooks=(maxima_local, maxima_reduced, scales))
            dve.wait_ge(s_scale, 1)
            with dve.Fori(8, 13, 2) as b:
                step(b, 0, weights=b - 8)
                step(b + 1, 1, weights=b - 7)
            for b, e in ((14, 6), (15, 7), (16, None), (17, None)):
                step(b, b % 2, weights=e)

            def result(t, u, e):
                dve.wait_ge(m_down, t + 1)
                V.scalar_tensor_tensor(YT[:, ds(t * SUB, SUB), :], bank[6 + u][:, 0:SUB * D].rearrange("p (s d) -> p s d", s=SUB),
                                       c2[:], spread(b2_sb[:, ds(e * D, D)].unsqueeze(1), 1, SUB),
                                       ALU.mult, ALU.add).then_inc(m_yraw, 1)
                dve.wait_ge(m_yraw, t + 1)
                y = YT[:, ds(t * SUB, SUB), :]
                V.tensor_tensor(y, y, spread(SLOT_ROWS[:, ds(t * SUB, SUB), D + 1:D + 2], 2, D), ALU.mult).then_inc(m_y, 1)

            def moe(t, u, before):
                if live(t, MOE_TILES):
                    dve.wait_ge(m_h, t + 1)
                    wait(dve, m_down, t - 1)
                    V.tensor_copy(Hs[:, u, 0, :], Hf[:, u, :]).then_inc(s_hi16, 1)
                    dve.wait_ge(s_hi16, t + 1)
                    V.tensor_tensor(Hs[:, u, 1, :], Hf[:, u, :], Hs[:, u, 0, :], ALU.subtract).then_inc(m_split, 1)
                if live(t - 1, MOE_TILES):
                    result(t - 1, 1 - u, before)
            e = experts(mybir.EngineType.DVE, 0)
            moe(0, 0, None)
            moe(1, 1, e[0])
            moe(2, 0, e[1])
            with dve.Fori(1, MOE_TILES // 2 - 1) as g:
                e = experts(mybir.EngineType.DVE, g)
                moe(2 * g + 1, 1, e[0])
                moe(2 * g + 2, 0, e[1])
            e = experts(mybir.EngineType.DVE, MOE_TILES // 2 - 1)
            moe(MOE_TILES - 1, 1, e[0])
            moe(MOE_TILES, 0, e[1])

            for g in range(4):
                dve.wait_ge(s_yb[g], 32)
                at = slice(FC * g, FC * (g + 1))
                V.tensor_tensor(X[:, at, :], X[:, at, :], YB[:, 0, at, :], ALU.add).then_inc(s_comb, 1)
                dve.wait_ge(s_comb, g + 1)
                V.tensor_tensor(X[:, at, :], X[:, at, :], YB[:, 1, at, :], ALU.add).then_inc(s_fin, 1)

        @block.tensor
        def _(pe):
            mm = nc.tensor.matmul

            def three(ps, a_hi, a_lo, b_hi, b_lo, first=True, last=True):
                mm(ps, a_lo, b_hi, start=first, stop=False)
                mm(ps, a_hi, b_lo, start=False, stop=False)
                return mm(ps, a_hi, b_hi, start=False, stop=last)

            pe.wait_ge(s_const, 1)
            pe.wait_ge(s_early, 16 * 8)
            nc.tensor.transpose(bank[3][:, 0:P], Wq_sb[:], ident[:])
            nc.tensor.transpose(bank[3][:, P:2 * P], Wk_sb[:], ident[:]).then_inc(s_wt, 1)
            pe.wait_ge(s_rb, 1)
            mm(bank[6][:], BQK[:, 0:P], RB, start=True, stop=True)
            mm(bank[7][:], BQK[:, P:2 * P], RB, start=True, stop=True)

            pe.wait_ge(s_router_w, 32)

            def transposes(g, u):
                pe.wait_ge(s_pxn, g + 1)
                wait(pe, s_pxT, g - 1)
                for i in range(RT):
                    last = nc.tensor.transpose(bank[u][:, i * P:(i + 1) * P], XN[:, u, i, :], ident[:])
                last.then_inc(s_pT, 1)

            def router(g, u):
                if live(g + 1, RG):
                    transposes(g + 1, 1 - u)
                pe.wait_ge(s_pxT, g + 1)
                wait(pe, s_pL, g - 1)
                for i in range(RT):
                    last = mm(bank[2 + u][:, i * E:(i + 1) * E], XTR[:, u, i * P:(i + 1) * P], Wr_sb[:], start=True, stop=True)
                last.then_inc(s_plog, 1)
            transposes(0, 0)
            router(0, 0)
            pe.wait_ge(s_wtc, 1)
            mm(bank[4][:], WT[:, 0:P], RB, start=True, stop=True)
            mm(bank[5][:], WT[:, P:2 * P], RB, start=True, stop=True).then_inc(s_fold, 1)
            for g in range(1, RG):
                router(g, g % 2)

            def passes(ps, bias_pass, pairs):
                yield lambda: mm(ps, *bias_pass, start=True, stop=False)
                for n, (a, b) in enumerate(pairs):
                    yield lambda a=a, b=b, n=n: mm(ps, a, b, start=False, stop=(n == 2))

            def kproj(j, u):
                at = slice(j * P, (j + 1) * P)
                hi, lo = xT_hi[:, u, at], xT_lo[:, u, at]
                return passes(psK[j][:], (pick3[:, 0:P], BIAS3[:, FEAT:2 * FEAT]),
                              ((lo, WkR_hi[:]), (hi, WkR_lo[:]), (hi, WkR_hi[:])))

            def qproj(c, u):
                at = slice(c * P, (c + 1) * P)
                return passes(psQ[c // 2][:, (c % 2) * NJ * P:(c % 2 + 1) * NJ * P], (BIAS3[:, at], pick3[:]),
                              ((WqR_lo[:, at], xT_hi[:, u, :]), (WqR_hi[:, at], xT_lo[:, u, :]),
                               (WqR_hi[:, at], xT_hi[:, u, :])))

            def step(b, u, hooks=None):
                if live(b + 1):
                    pe.wait_ge(xn_ready, b + 2)
                    wait(pe, xlo_ready, b + 1)
                    wait(pe, xhi_ready, b + 1)
                    for j in range(NJ):
                        last = nc.tensor.transpose(psT[:, j * P:(j + 1) * P], XN[:, 1 - u, j, :], ident[:])
                    last.then_inc(xt_done, 1)
                if live(b):
                    pe.wait_ge(xhi_ready, b + 1)
                    pe.wait_ge(xlo_ready, b + 1)
                if live(b - 1):
                    pe.wait_ge(v_ready, b)
                    pe.wait_ge(kf_ready, 2 * b)
                for j in range(NJ):
                    wide = kproj(j, u) if live(b) else iter(())
                    for c in range(NC):
                        if live(b):
                            last = next(wide)()
                            if c == NC - 1:
                                last.then_inc(k_done, 1)
                        if live(b - 1):
                            ch, i = 2 * j + c // 2, c % 2
                            last = mm(psKV[:, ch, :], KF[:, 1 - u, i, ch * P:(ch + 1) * P], VA[:, 1 - u, i, ch, :],
                                      start=(i == 0), stop=(i == NJ - 1))
                            if j == NJ - 1 and c == NC - 1:
                                last.then_inc(kv_done, 1)
                if live(b - 2):
                    pe.wait_ge(o_ready, b - 1)
                    wait(pe, base_ready, b - 2)
                    ov = O_sb[:].rearrange("p c w -> p (c w)")
                    for j in range(NJ):
                        last = nc.tensor.transpose(psOA[:, j * P:(j + 1) * P], ov[:, j * P:(j + 1) * P], ident[:])
                    last.then_inc(ot_done, 1)
                if hooks:
                    hooks[0]()
                if live(b):
                    wait(pe, qf_ready, 2 * b - 1)
                    for c in range(2):
                        for product in qproj(c, u):
                            last = product()
                    last.then_inc(q_done, 1)
                    wait(pe, bd_ready, b)
                    for j in range(NJ):
                        at, to = slice(j * P, (j + 1) * P), psV[:, j * D:(j + 1) * D]
                        mm(to, pick3[:, 0:P], BIAS3[:, 2 * FEAT:2 * FEAT + D], start=True, stop=False)
                        last = three(to, xT_hi[:, u, at], xT_lo[:, u, at], Wv_hi[:], Wv_lo[:], first=False)
                    last.then_inc(v_done, 1)
                    wait(pe, qf_ready, 2 * b)
                if hooks:
                    hooks[1]()
                if live(b - 1):
                    pe.wait_ge(bd_ready, b)
                    pe.wait_ge(qf_ready, 2 * b)
                    wait(pe, o_ready, b - 1)
                    if hooks:
                        pe.wait_ge(s_mread, 1)
                wide = [p for c in (2, 3) for p in qproj(c, u)] if live(b) else []
                for n in range(NJ * NC):
                    if wide:
                        last = wide[n]()
                        if n == NJ * NC - 1:
                            last.then_inc(q_done, 1)
                    if live(b - 1):
                        j, c = n // NC, n % NC
                        last = mm(psOut[:, n, :], QF[:, 1 - u, c, j * P:(j + 1) * P], BD[:, c, :], start=True, stop=True)
                        if n == NJ * NC - 1:
                            last.then_inc(out_done, 1)
                if live(b - 2):
                    pe.wait_ge(ot_ready, b - 1)
                    for j in range(NJ):
                        to = psOA[:, (NJ + j) * P:(NJ + j + 1) * P]
                        mm(to, pick3[:, 0:P], BIAS3[:, 2 * FEAT + D:NBIAS], start=True, stop=False)
                        last = mm(to, OT_sb[:, j * P:(j + 1) * P], Wo_sb[:], start=False, stop=True)
                    last.then_inc(att_done, 1)

            def transpose_maxima():
                pe.wait_ge(s_mx, 1)
                nc.tensor.transpose(psO[0:3, 384:512], mx3[:], ident[:]).then_inc(s_mxT, 1)

            def broadcast_maxima():
                pe.wait_ge(s_m3, 1)
                mm(psO[:, 320:323], m3b[0:3, :], ident[0:3, 0:3], start=True, stop=True).then_inc(s_mb, 1)

            pe.wait_ge(s_pL, RG)
            pe.wait_ge(s_bias, 1)
            pe.wait_ge(s_late, 16 * 3)
            step(-1, 1)
            step(0, 0)
            pe.wait_ge(s_oneh, 1)
            mm(bank[1][:], upper[:], ONEHOT16, start=True, stop=True)
            mm(bank[7][:], ones[:], ONEHOT16, start=True, stop=True).then_inc(s_pfx, 1)

            pe.wait_ge(s_slots, 1)
            step(1, 1)
            step(2, 0)
            steps(pe, 3, 6, step)
            step(7, 1, hooks=(transpose_maxima, broadcast_maxima))
            steps(pe, 8, 13, step)
            for b in (14, 15, 16, 17):
                step(b, b % 2)

            words = SLOT_ROWS[:].bitcast(f16)

            def rows(t, u):
                wait(pe, m_xT, t - 1)
                for part in range(2):
                    for i in range(SUB):
                        at = (part * SUB + i) * P // 2
                        last = nc.tensor.transpose(
                            bank[u][:, at:at + P // 2].bitcast(f16),
                            words[:, ds(t * SUB + i, 1), part * D:(part + 1) * D].rearrange("p a d -> p (a d)"), identh[:])
                last.then_inc(m_T, 1)

            def up(t, u, e):
                pe.wait_ge(m_xT, t + 1)
                wait(pe, m_h, t - 1)
                xh = XTS[:, u, 0:TS // 2].bitcast(f16)
                xl = XTS[:, u, TS // 2:TS].bitcast(f16)
                for c in range(HCH):
                    to, at = up_bank(u, c), ds(e * HID + c * P, P)
                    mm(to, W1l[:, at], xh, start=True, stop=False)
                    mm(to, W1h[:, at], xl, start=False, stop=False)
                    last = mm(to, W1h[:, at], xh, start=False, stop=True)
                last.then_inc(m_up, 1)

            def down(t, u, e):
                pe.wait_ge(m_split, t + 1)
                wait(pe, m_y, t - 1)
                for i in range(SUB):
                    to = bank[6 + u][:, i * D:(i + 1) * D]
                    for c in range(HCH):
                        at = ds(e * HID + c * P, P)
                        rows_at = slice(c * TS + i * P, c * TS + (i + 1) * P)
                        hh, hl = Hs[:, u, 0, rows_at], Hs[:, u, 1, rows_at]
                        mm(to, hl, W2h[:, at], start=(c == 0), stop=False)
                        mm(to, hh, W2l[:, at], start=False, stop=False)
                        last = mm(to, hh, W2h[:, at], start=False, stop=(c == HCH - 1))
                last.then_inc(m_down, 1)

            def moe(t, u, before, e):
                if live(t + 1, MOE_TILES):
                    rows(t + 1, 1 - u)
                if live(t, MOE_TILES):
                    up(t, u, e)
                if live(t - 1, MOE_TILES):
                    down(t - 1, 1 - u, before)

            def loop(first, last):
                with pe.Fori(first, last + 1) as g:
                    e = experts(mybir.EngineType.PE, g)
                    moe(2 * g + 1, 1, e[0], e[1])
                    moe(2 * g + 2, 0, e[1], e[2])

            pe.wait_ge(base_ready, NBATCH)
            pe.wait_ge(s_wsplit, E)
            pe.wait_ge(s_load[0], 16)
            rows(0, 0)
            e = experts(mybir.EngineType.PE, 0)
            moe(0, 0, None, e[0])
            moe(1, 1, e[0], e[1])
            moe(2, 0, e[1], e[2])
            first = (FIRST_LOAD - 2) // 2 - 1
            loop(1, first)
            pe.wait_ge(s_load[1], 16)
            loop(first + 1, MOE_TILES // 2 - 2)
            e = experts(mybir.EngineType.PE, MOE_TILES // 2 - 1)
            moe(MOE_TILES - 1, 1, e[0], e[1])
            moe(MOE_TILES, 0, e[1], None)


_INS = ["L0_attn_x", "L0_attn_Wq", "L0_attn_bq", "L0_attn_Wk", "L0_attn_bk", "L0_attn_Wv", "L0_attn_bv",
        "L0_attn_Wo", "L0_attn_bo", "L0_attn_random_matrix", "L0_ffn_Wr", "L0_ffn_br", "L0_ffn_W1",
        "L0_ffn_b1", "L0_ffn_W2", "L0_ffn_b2"]


def kernel(**inputs):
    import numpy as _np
    import concourse.bacc as _bacc
    from concourse import mybir as _mybir
    from concourse.bass_utils import run_bass_kernel_spmd as _run

    nc = _bacc.Bacc("TRN2", target_bir_lowering=False, num_devices=1)
    arrays, args = {}, []
    for name in _INS:
        a = _np.ascontiguousarray(inputs[name])
        arrays[f"in_{name}"] = a
        args.append(nc.dram_tensor(f"in_{name}", a.shape, _mybir.dt.from_np(a.dtype), kind="ExternalInput").ap())
    f32 = _mybir.dt.float32
    out = nc.dram_tensor("out_0", (NBATCH, NJ * P, D), f32, kind="ExternalOutput").ap()
    rows_dram = nc.dram_tensor("slot_rows", (SLOTS, ROWW), f32, kind="Internal").ap()
    y_dram = nc.dram_tensor("expert_results", (TOPK * T, D), f32, kind="Internal").ap()
    program(nc, *args, out, rows_dram, y_dram)
    r = _run(nc, [arrays], core_ids=[0])
    return r.results[0]["out_0"]
```

```python
import concourse.bass as bass
from concourse import mybir
from contextlib import ExitStack

P = 128
NBATCH = 16
NJ = 2
D = 128
NT = NBATCH * NJ
T = NT * P
HEADS, HD, M = 16, 8, 32
FEAT = HEADS * M
NC = FEAT // P
HC = P // M
KVW = HC * HD + HC
E, HID, TOPK = 8, 512, 2
HCH = HID // P
RT = 4
RG = NT // RT
DUPS = 4
SUB = 2
TS = SUB * P
TS_LOG2 = TS.bit_length() - 1
GROUP = 8
MOE_TILES = (TOPK * T + E * (TS - 1)) // TS
TURNS = -(-MOE_TILES // GROUP)
ROOM = TURNS * GROUP
SLOTS = ROOM * TS
ROWW = D + 2
PRE = 4
NO_ROW = TOPK * T
OUT_CHUNKS = 8
EPS = 1e-5
NORM_MIN = 1e-6 * 256.0
NEG = -3.0e38


def program(nc, x, wq, bq, wk, bk, wv, bv, wo, bo, rm, wr, br, w1, b1, w2, b2, out, rows_dram, y_dram):
    f32, f32r, f16, bf16 = mybir.dt.float32, mybir.dt.float32r, mybir.dt.float16, mybir.dt.bfloat16
    i32 = mybir.dt.int32
    ALU, ACT, AX = mybir.AluOpType, mybir.ActivationFunctionType, mybir.AxisListType
    ds = bass.ds

    with ExitStack() as ctx:
        def sb(name, shape, dt=f32):
            return ctx.enter_context(nc.sbuf_tensor(name, shape, dt))

        def sem(name):
            return ctx.enter_context(nc.semaphore(name))

        X = sb("X", [P, NT, D])
        SLOT_ROWS = sb("SLOT_ROWS", [P, ROOM * SUB, ROWW])
        XS = SLOT_ROWS[:, 0:TOPK * NT, :].rearrange("p (k t) w -> p k t w", k=TOPK)
        YB = SLOT_ROWS[:, :, :].rearrange("p t w -> p (t w)")[:, 0:TOPK * NT * D].rearrange(
            "p (k t d) -> p k t d", k=TOPK, d=D)
        WRAW = sb("WRAW", [P, ROOM * SUB * D])
        W1raw = WRAW[:, 0:E * HID].rearrange("p (e h) -> p e h", e=E)
        W2raw = WRAW[:, E * HID:2 * E * HID].rearrange("p (e h) -> p e h", e=E)
        YT = WRAW[:, :].rearrange("p (t d) -> p t d", d=D)
        W1h, W1l = sb("W1h", [P, E, HCH, P], f16), sb("W1l", [P, E, HCH, P], f16)
        W2h, W2l = sb("W2h", [P, E, HCH, D], f16), sb("W2l", [P, E, HCH, D], f16)
        PREFILL = sb("PREFILL", [P, PRE, ROWW])
        XN = sb("XN", [P, 2, RT, D])
        xT_hi, xT_lo = sb("xT_hi", [P, 2, NJ * P], f32r), sb("xT_lo", [P, 2, NJ * P], f32r)
        EK = sb("EK", [P, NJ, FEAT])
        KF = sb("KF", [P, 2, NJ, FEAT])
        EQ = sb("EQ", [P, NC, NJ * P])
        QF = sb("QF", [P, 2, NC, NJ * P])
        NBIAS = FEAT + 2 * D
        FOLD = W1h[:, :, :, :].rearrange("p e c a -> p (e c a)").bitcast(f32)[:, 0:2 * FEAT].rearrange(
            "p (a n) -> p a n", a=2)
        B_REST = W1l[:, :, :, :].rearrange("p e c a -> p (e c a)").bitcast(f32)[:, 0:NBIAS]
        RB = EK[:, 0, :]
        WT = EK[:, 1, 0:2 * P]
        BK_REP = EK[:, 1, 2 * P:3 * P]
        XTR = EQ[:, :, :].rearrange("p c n -> p (c n)").rearrange("p (u n) -> p u n", u=2)
        KFflat = KF[:, :, :, :].rearrange("p a b c -> p (a b c)")
        QFflat = QF[:, :, :, :].rearrange("p a b c -> p (a b c)")
        B_REP = KFflat[:, 0:NBIAS]
        TMP = WRAW[:, 2 * E * HID:]
        CH = E * TOPK * NT
        ONEHOT = TMP[:, 0:CH].rearrange("p (e k t) -> p e k t", e=E, k=TOPK)
        ONEHOT16 = TMP[:, CH:CH * 3 // 2].bitcast(bf16)
        CUM = TMP[:, CH * 3 // 2:CH * 5 // 2]
        SLOTM = TMP[:, CH * 5 // 2:CH * 7 // 2]
        Hf = KFflat.rearrange("p (u n) -> p u n", u=2)
        Hs = QFflat.bitcast(f16).rearrange("p (u s n) -> p u s n", u=2, s=2)
        BIAS3 = sb("BIAS3", [P, NBIAS], bf16)
        pick3 = sb("pick3", [P, P], bf16)
        WqR_hi, WqR_lo = sb("WqR_hi", [P, FEAT], f32r), sb("WqR_lo", [P, FEAT], f32r)
        WkR_hi, WkR_lo = sb("WkR_hi", [P, FEAT], f32r), sb("WkR_lo", [P, FEAT], f32r)
        Wv_hi, Wv_lo = sb("Wv_hi", [P, D], f32r), sb("Wv_lo", [P, D], f32r)
        Wq_sb, Wk_sb, Wv_sb, Wo_sb = (sb(n, [P, D]) for n in ("Wq_sb", "Wk_sb", "Wv_sb", "Wo_sb"))
        Wr_sb, br_sb = sb("Wr_sb", [P, E]), sb("br_sb", [P, E])
        R_sb = sb("R_sb", [P, M])
        bqk_sb = sb("bqk_sb", [P, 2])
        q_bias1, q_nbias = sb("q_bias1", [P, NC]), sb("q_nbias", [P, NC])
        b1_sb, b1s = sb("b1_sb", [P, E, HCH]), sb("b1s", [P, E, HCH])
        b2_sb = sb("b2_sb", [P, E, D])
        ident, identh = sb("ident", [P, P]), sb("identh", [P, P], f16)
        upper = sb("upper", [P, P], bf16)
        ones = sb("ones", [P, P], bf16)
        ones32 = sb("ones32", [P, 512])
        head_mask = sb("head_mask", [P, HEADS])
        bd_mask = sb("bd_mask", [P, KVW])
        rank8 = sb("rank8", [P, E])
        tile_no = sb("tile_no", [P, ROOM])
        stats = sb("stats", [P, NT, 6])
        ln = sb("ln", [P, 8, NT])
        mean, rstd = ln[:, 0, :], ln[:, 1, :]
        L, L2, EQM = sb("L", [P, NT, E]), sb("L2", [P, NT, E]), sb("EQM", [P, NT, E])
        top = sb("top", [P, TOPK, NT])
        best = sb("best", [P, TOPK, NT])
        gates = sb("gates", [P, TOPK, NT])
        gtmp = sb("gtmp", [P, NT])
        small = sb("small", [P, 7, E])
        smalli = sb("smalli", [P, 2, E], i32)
        slot_f, slot_i = sb("slot_f", [P, TOPK * NT]), sb("slot_i", [P, TOPK * NT], i32)
        ended = sb("ended", [P, ROOM, E])
        expert_f = sb("expert_f", [P, ROOM])
        expert_i = sb("expert_i", [P, ROOM], i32)
        VA = sb("VA", [P, 2, NJ, NC, KVW])
        BD = sb("BD", [P, NC, KVW])
        den = sb("den", [P, NJ * NC, HC])
        O_sb, OT_sb = sb("O_sb", [P, NJ * NC, HC * HD]), sb("OT_sb", [P, NJ * P])
        mx1, mx2, mx3 = sb("mx1", [P, 4]), sb("mx2", [P, 4]), sb("mx3", [P, 3])
        m3, m3b = sb("m3", [P, 1]), sb("m3b", [P, P])
        bound = sb("bound", [P, 2])
        fld, scl, inv = sb("fld", [P, 2], i32), sb("scl", [P, 2], i32), sb("inv", [P, 2], i32)
        c2 = sb("c2", [P, 1])
        neg1 = sb("neg1", [P, 1])
        XTS = sb("XTS", [P, 2, TS])

        bank = [ctx.enter_context(nc.psum_tensor(f"bank{i}", [P, 512], f32)) for i in range(8)]
        psT, psOA, psK, psQ, psVK, psO = bank[0], bank[1], bank[2:4], bank[4:6], bank[6], bank[7]
        psMaxT, psMax = psT[0:3, 512 - P:512], psT[:, 320:323]
        psV = psVK[:, 160:160 + NJ * D]
        psKV = psVK[:, 0:NC * KVW].rearrange("p (c w) -> p c w", c=NC)
        psOut = psO[:, 0:NJ * NC * KVW].rearrange("p (c w) -> p c w", w=KVW)

        s_router_w, s_early, s_late, s_w = (sem(n) for n in (
            "router_weights", "early_weights", "late_weights", "expert_weights"))
        s_x = [sem(f"x_chunk{i}") for i in range(4)]
        s_const, s_pre, s_prefilled = sem("constants_made"), sem("prefill_made"), sem("slots_prefilled")
        s_wt, s_wtc, s_rb, s_fold, s_folded, s_bias = (sem(n) for n in (
            "w_transposed", "w_transposed_copied", "rb_built", "folded", "fold_read", "bias_parts_made"))
        s_var, s_sqrt = sem("variance_ready"), sem("sqrt_ready")
        s_pxn, s_phi, s_plo, s_pT, s_pxT, s_plog, s_pL = (sem(n) for n in (
            "router_rows_normalised", "router_hi_written", "router_lo_written", "router_transposed",
            "router_transposed_copied", "router_logits_done", "router_logits_read"))
        s_dup, s_gates = sem("rows_duplicated"), sem("gates_written")
        s_gd, s_gexp, s_oneh, s_pfx, s_pfxr, s_slots = (sem(n) for n in (
            "gate_difference", "gate_exp", "onehot_ready", "prefixes_done", "prefixes_read", "slots_ready"))
        s_bpart, s_brest = sem("bias_part"), sem("bias_rest")
        s_scat = sem("rows_scattered")
        s_load = sem("slots_loaded")
        s_dve, s_pool, s_act = sem("dve_step"), sem("pool_step"), sem("act_step")
        (xn_ready, xt_done, xhi_ready, xlo_ready, k_done, v_done, q_done, ek_ready, kf_ready, eq_ready,
         qf_ready, v_ready, kv_done, bd_ready, out_done, o_ready, ot_done, ot_ready, att_done,
         base_ready) = (sem(n) for n in (
             "xn_ready", "xt_done", "xhi_ready", "xlo_ready", "k_done", "v_done", "q_done", "ek_ready",
             "kf_ready", "eq_ready", "qf_ready", "v_ready", "kv_done", "bd_ready", "out_done", "o_ready",
             "ot_done", "ot_ready", "att_done", "base_ready"))
        s_mx, s_mxT, s_m3, s_mb, s_scale, s_wsplit, s_whi = (sem(n) for n in (
            "weight_maxima", "maxima_transposed", "maxima_reduced", "maxima_broadcast", "scales_ready",
            "expert_weights_lo", "expert_weights_hi"))
        m_yraw = sem("y_ungated")
        (m_T, m_xT, m_up, m_h, m_split, m_down, m_y) = (sem(n) for n in (
            "slot_rows_transposed", "slot_rows_copied", "up_done", "hidden_ready", "hidden_split",
            "down_done", "y_ready"))
        s_mread = sem("maxima_read")
        s_ysc = sem("y_scattered")
        s_yb = [sem(f"y_back{i}") for i in range(OUT_CHUNKS)]
        s_fin, s_comb, s_norm, s_hi16 = sem("chunk_combined"), sem("tile_combined"), sem("norm_step"), sem("hidden_hi")
        s_out = sem("out_written")

        block = ctx.enter_context(nc.Block())
        FC, OC = NT // 4, NT // OUT_CHUNKS

        def wait(eng, semaphore, value):
            if not isinstance(value, int) or value > 0:
                eng.wait_ge(semaphore, value)

        def spread(ap, dim, n):
            return ap.broadcast_to([n if i == dim else size for i, size in enumerate(ap.shape)])

        def live(b, n=NBATCH):
            return not isinstance(b, int) or 0 <= b < n

        def steps(eng, first, last, body):
            with eng.Fori(first, last, 2) as b:
                body(b, first % 2)
                body(b + 1, (first + 1) % 2)

        def experts(engine, first, n):
            return list(nc.values_load_multi_w_load_instructions(
                expert_i[0:1, ds(first, n)], engines=[engine], min_val=0, max_val=E - 1,
                skip_runtime_bounds_check_because="the program clamps them to E - 1")[1])

        def slot_tile(v, g, k, i=0, n=SUB):
            v = v.rearrange("p (g q) w -> p g q w", q=GROUP * SUB)[:, ds(g + k // GROUP, 1)]
            at = k % GROUP * SUB + i
            return v[:, :, at:at + n, :].rearrange("p a q w -> p (a q) w")

        def up_bank(u, c):
            return bank[2 + 2 * u + c // 2][:, (c % 2) * TS:(c % 2 + 1) * TS]

        def rows_bank(t, u):
            return bank[6] if isinstance(t, int) and t == 1 else bank[u]

        def x_view(dram):
            return dram.rearrange("b (p j) d -> p b j d", j=NJ)

        @block.sync
        def _(sp):
            for g in range(4):
                sp.dma_start(X[:, FC * g:FC * (g + 1), :].rearrange("p (b j) d -> p b j d", j=NJ),
                             x_view(x)[:, g * FC // NJ:(g + 1) * FC // NJ]).then_inc(s_x[g], 16)
            sp.wait_ge(s_pre, 1)
            sp.wait_ge(s_x[3], 16)
            pre = rows_dram.rearrange("(g p t) w -> g p t w", p=P, t=PRE)
            for g in range(SLOTS // (P * PRE)):
                sp.dma_start(pre[g], PREFILL[:]).then_inc(s_prefilled, 16)
            sp.dma_start(W1raw, w1.rearrange("e d h -> d e h")).then_inc(s_w, 16)
            sp.dma_start(W2raw.rearrange("p e (c o) -> p e c o", c=HCH),
                         w2.rearrange("e (p c) o -> p e c o", c=HCH)).then_inc(s_w, 16)
            sp.wait_ge(s_scat, 16 * TOPK * NT)
            slots = rows_dram.rearrange("(t p) w -> p t w", p=P)
            sp.dma_start(SLOT_ROWS[:, 0:MOE_TILES * SUB, :], slots[:, 0:MOE_TILES * SUB]).then_inc(s_load, 16)
            sp.wait_ge(s_ysc, 16 * MOE_TILES * SUB)
            yv = y_dram.rearrange("(k p t) d -> p k t d", k=TOPK, p=P)
            for g in range(OUT_CHUNKS):
                for k in range(TOPK):
                    sp.dma_start(YB[:, k, OC * g:OC * (g + 1), :], yv[:, k, OC * g:OC * (g + 1)]).then_inc(s_yb[g], 16)
            for g in range(OUT_CHUNKS):
                sp.wait_ge(s_fin, g + 1)
                sp.dma_start(x_view(out)[:, g * OC // NJ:(g + 1) * OC // NJ],
                             X[:, OC * g:OC * (g + 1), :].rearrange("p (b j) d -> p b j d", j=NJ)).then_inc(s_out, 16)
            sp.wait_ge(s_out, 16 * OUT_CHUNKS)

        @block.gpsimd
        def _(pool):
            count = [0]

            def link(ins):
                count[0] += 1
                ins.then_inc(s_pool, 1)
                pool.wait_ge(s_pool, count[0])

            def keep(t, op, base, pattern, mult):
                link(nc.gpsimd.affine_select(out=t, in_=t, compare_op=op, fill=0.0, base=base,
                                             pattern=pattern, channel_multiplier=mult))

            for t in (ident, upper, ones, pick3, ones32, bd_mask, head_mask, VA):
                nc.gpsimd.memset(t[:], 1.0)
            link(nc.gpsimd.memset(PREFILL[:], 0.0))
            nc.gpsimd.memset(PREFILL[:].bitcast(i32)[:, :, D], NO_ROW).then_inc(s_pre, 1)
            keep(ident[:], ALU.is_equal, 0, [[1, P]], -1)
            link(nc.gpsimd.tensor_copy(identh[:], ident[:]))
            keep(head_mask[:], ALU.is_ge, 0, [[-HD, HEADS]], 1)
            keep(head_mask[:], ALU.is_ge, HD - 1, [[HD, HEADS]], -1)
            for v, inner in ((bd_mask[:, 0:HC * HD], [[0, HD]]), (bd_mask[:, HC * HD:KVW], [])):
                keep(v, ALU.is_ge, 0, [[-M, HC]] + inner, 1)
                keep(v, ALU.is_ge, M - 1, [[M, HC]] + inner, -1)
            keep(upper[:], ALU.is_gt, 0, [[1, P]], -1)
            for row in (0, 64, 96):
                V3 = pick3[row:row + 32, :]
                keep(V3, ALU.is_equal, 0, [[0, P]], 1)
            keep(pick3[32:64, :], ALU.is_gt, 0, [[0, P]], -1)
            nc.gpsimd.iota(rank8[:], pattern=[[-1, E]], base=E, channel_multiplier=0,
                           allow_small_or_imprecise_dtypes=True)
            link(nc.gpsimd.iota(tile_no[:], pattern=[[1, ROOM]], base=0, channel_multiplier=0,
                                allow_small_or_imprecise_dtypes=True))
            nc.gpsimd.iota(XS.bitcast(i32)[:, :, :, D], pattern=[[T, TOPK], [1, NT]], base=0,
                           channel_multiplier=NT).then_inc(s_const, 1)

            G = nc.gpsimd
            pool.wait_ge(s_early, 16 * 8)
            G.tensor_copy(BK_REP, spread(bqk_sb[:, 1:2], 1, P))
            G.tensor_tensor(RB.rearrange("p (h m) -> p h m", h=HEADS), spread(R_sb[:].unsqueeze(1), 1, HEADS),
                            spread(head_mask[:].unsqueeze(2), 2, M), ALU.mult).then_inc(s_rb, 1)
            pool.wait_ge(s_folded, 1)
            G.tensor_tensor(WqR_lo[:], FOLD[:, 0, :], WqR_hi[:].bitcast(f32), ALU.subtract)
            G.tensor_tensor(WkR_lo[:], FOLD[:, 1, :], WkR_hi[:].bitcast(f32), ALU.subtract)
            pool.wait_ge(s_folded, 2)
            G.tensor_tensor(Wv_lo[:], Wv_sb[:], Wv_hi[:].bitcast(f32), ALU.subtract)
            for n in range(2):
                pool.wait_ge(s_bpart, n + 1)
                G.tensor_tensor(B_REST, B_REST if n else B_REP, BIAS3[:], ALU.subtract).then_inc(s_brest, 1)
                pool.wait_ge(s_brest, n + 1)
            pool.wait_ge(s_gates, 1)
            pool.wait_ge(s_slots, 1)
            pool.wait_ge(s_prefilled, 16 * (SLOTS // (P * PRE)))
            for c in range(TOPK * NT):
                if c == NT:
                    pool.wait_ge(s_dup, DUPS)
                nc.gpsimd.indirect_dma_start(
                    rows_dram, bass.IndirectOffsetOnAxis(ap=slot_i[:, c:c + 1], axis=0),
                    XS[:, c // NT, c % NT, :], None).then_inc(s_scat, 16)
            ids = SLOT_ROWS[:].bitcast(i32)
            pool.wait_ge(s_load, 16)
            for t in range(MOE_TILES * SUB):
                if t % SUB == 0:
                    pool.wait_ge(m_y, t // SUB + 1)
                nc.gpsimd.indirect_dma_start(
                    y_dram, bass.IndirectOffsetOnAxis(ap=ids[:, t, D:D + 1], axis=0), YT[:, t, :], None,
                    bounds_check=NO_ROW - 1, oob_is_err=False).then_inc(s_ysc, 16)

        @block.scalar
        def _(act):
            for dst, src in ((Wr_sb[:], wr), (br_sb[:], br.partition_broadcast(P))):
                act.dma_start(dst, src).then_inc(s_router_w, 16)
            for dst, src in ((Wq_sb[:], wq), (Wk_sb[:], wk), (bqk_sb[:, 0:1], bq.unsqueeze(1)),
                             (bqk_sb[:, 1:2], bk.unsqueeze(1)), (Wv_sb[:], wv)):
                act.dma_start(dst, src).then_inc(s_early, 16)
            act.dma_start(R_sb[:], bass.AP(rm.tensor, 0, [[0, P // HD], [M, HD], [1, M]])).then_inc(s_early, 16)
            act.dma_start(B_REP[:, FEAT:FEAT + D], bv.partition_broadcast(P)).then_inc(s_early, 16)
            act.dma_start(B_REP[:, FEAT + D:NBIAS], bo.partition_broadcast(P)).then_inc(s_early, 16)
            act.dma_start(Wo_sb[:], wo).then_inc(s_late, 16)
            act.dma_start(b1_sb[:], b1.rearrange("e (p c) -> p e c", c=HCH)).then_inc(s_late, 16)
            act.dma_start(b2_sb[:].rearrange("p e o -> p (e o)"), b2.rearrange("e o -> (e o)").partition_broadcast(P)).then_inc(s_late, 16)

            act.wait_ge(s_wt, 1)
            nc.scalar.copy(WT, bank[3][:, 0:2 * P]).then_inc(s_wtc, 1)
            act.wait_ge(s_var, 1)
            nc.scalar.activation(ln[:, 3, :], ln[:, 2, :], ACT.Sqrt).then_inc(s_sqrt, 1)

            def router(g, u):
                act.wait_ge(s_pxn, g + 1)
                nc.scalar.copy(XS[:, 0, ds(g * RT, RT), 0:D // 2].bitcast(f16), XN[:, u]).then_inc(s_phi, 1)
                act.wait_ge(s_pT, g + 1)
                wait(act, s_plog, g - 1)
                nc.scalar.copy(XTR[:, u, :], bank[u][:]).then_inc(s_pxT, 1)

            def dup(i):
                act.wait_ge(s_plo, RG)
                at = slice(i * NT // DUPS, (i + 1) * NT // DUPS)
                nc.scalar.copy(XS[:, 1, at, 0:D], XS[:, 0, at, 0:D]).then_inc(s_dup, 1)

            def folded_weights():
                act.wait_ge(s_fold, 1)
                nc.scalar.copy(WqR_hi[:], bank[4][:])
                nc.scalar.copy(WkR_hi[:], bank[5][:])
                nc.scalar.copy(FOLD[:, 0, :], bank[4][:])
                nc.scalar.copy(FOLD[:, 1, :], bank[5][:]).then_inc(s_folded, 1)

            def folded_biases():
                act.wait_ge(s_fold, 2)
                nc.scalar.activation(q_bias1[:], bank[6][:, 0:NC], ACT.Identity, bias=ones32[:, 0:1])
                nc.scalar.activation(q_nbias[:], bank[6][:, 0:NC], ACT.Copy, scale=-1.0)
                nc.scalar.activation(B_REP[:, 0:FEAT], bank[7][:], ACT.Identity, bias=ones32[:, 0:1])
                act.wait_ge(s_early, 16 * 8)
                nc.scalar.copy(Wv_hi[:], Wv_sb[:]).then_inc(s_folded, 1)

            def bias_part(n):
                if n:
                    act.wait_ge(s_brest, n)
                rows = slice((0, 64, 96)[n], P)
                nc.scalar.copy(BIAS3[rows, :], (B_REST if n else B_REP)[rows, :]).then_inc(s_bpart if n < 2 else s_bias, 1)

            for g in range(RG):
                router(g, g % 2)
                if g == 0:
                    folded_weights()
                if g == 2:
                    folded_biases()
                    act.wait_ge(s_folded, 2)
                if g in (3, 5, 7):
                    bias_part(g // 2 - 1)

            def hi_part(b):
                if not live(b):
                    return
                u = parity(b)
                act.wait_ge(xt_done, b + 1)
                wait(act, q_done, 2 * b - 2)
                nc.scalar.copy(xT_hi[:, u, :], psT[:, 0:NJ * P]).then_inc(xhi_ready, 1)

            par = [0]

            def parity(b):
                return b % 2 if isinstance(b, int) else par[0]

            def step(b, u, extra=None):
                par[0] = 1 - u
                hi_part(b + 1)
                par[0] = u
                if live(b):
                    for j in range(NJ):
                        act.wait_ge(k_done, 2 * b + j + 1)
                        wait(act, kf_ready, 2 * b - 1 + j)
                        nc.scalar.activation(EK[:, j, :], psK[j][:], ACT.Exp, bias=neg1[:, 0:1]).then_inc(ek_ready, 1)
                if live(b - 2):
                    act.wait_ge(ot_done, b - 1)
                    wait(act, att_done, b - 2)
                    nc.scalar.copy(OT_sb[:], psOA[:, 0:NJ * P]).then_inc(ot_ready, 1)
                if live(b):
                    for h in range(2):
                        act.wait_ge(q_done, 2 * b + h + 1)
                        wait(act, qf_ready, 2 * b - 1 + h)
                        for c in (2 * h, 2 * h + 1):
                            last = nc.scalar.activation(EQ[:, c, :], psQ[h][:, (c % 2) * NJ * P:(c % 2 + 1) * NJ * P],
                                                        ACT.Relu, bias=q_nbias[:, c:c + 1], scale=-1.0)
                        last.then_inc(s_act, 1)
                        act.wait_ge(s_act, 2 * b + h + 1)
                        nc.scalar.activation(EQ[:, 2 * h:2 * h + 2, :], EQ[:, 2 * h:2 * h + 2, :], ACT.Exp,
                                             scale=-1.0).then_inc(eq_ready, 1)
                        if h == 0:
                            act.wait_ge(v_done, b + 1)
                            wait(act, kv_done, b - 1)
                            nc.scalar.copy(VA[:, u, :, :, 0:HC * HD],
                                           psV.rearrange("p (j c w) -> p j c w", j=NJ, c=NC)).then_inc(v_ready, 1)
                            if extra:
                                extra()
                elif extra:
                    extra()

            def split_weights(e):
                for raw, hi, s in ((W1raw[:, ds(e, 1), :].rearrange("p e (a c) -> p (e c) a", c=HCH), W1h, 0),
                                   (W2raw[:, ds(e, 1), :].rearrange("p e (c a) -> p (e c) a", c=HCH), W2h, 1)):
                    nc.scalar.activation(hi[:, ds(e, 1)].rearrange("p e c a -> p (e c) a"), raw,
                                         ACT.Copy, scale=scl[:].bitcast(f32)[:, s:s + 1]).then_inc(s_whi, 1)

            def gate_exp():
                act.wait_ge(s_gd, 1)
                nc.scalar.activation(gtmp[:], gtmp[:], ACT.Exp).then_inc(s_gexp, 1)
                dup(2)

            def copy_rows(t, u):
                act.wait_ge(m_T, t + 1)
                wait(act, m_up, t - 1)
                nc.scalar.copy(XTS[:, u, :], rows_bank(t, u)[:, 0:TS]).then_inc(m_xT, 1)

            def relus(g, k, e):
                t, u = GROUP * g + k, k % 2
                act.wait_ge(m_up, t + 1)
                wait(act, m_split, t - 1)
                for c in range(HCH):
                    last = nc.scalar.activation(Hf[:, u, c * TS:(c + 1) * TS], up_bank(u, c), ACT.Relu,
                                                bias=b1s[:, ds(e, 1), c:c + 1].rearrange("p a c -> p (a c)"))
                last.then_inc(m_h, 1)

            step(-1, 1)
            for b, extra in enumerate((lambda: dup(0), gate_exp, lambda: dup(1), lambda: dup(3))):
                step(b, b % 2, extra)
            steps(act, 4, 7, step)
            step(8, 0)
            act.wait_ge(s_scale, 1)
            step(9, 1, lambda: split_weights(0))
            with act.Fori(10, 13, 2) as b:
                step(b, 0, lambda: split_weights(b - 9))
                step(b + 1, 1, lambda: split_weights(b - 8))
            step(14, 0, lambda: split_weights(5))
            split_weights(6)
            step(15, 1, lambda: split_weights(7))
            copy_rows(0, 0)
            step(16, 0)
            copy_rows(1, 1)
            relus(0, 0, experts(mybir.EngineType.Activation, 0, 1)[0])
            step(17, 1)
            copy_rows(2, 0)

            def turn(g, n=GROUP, first=0):
                e = experts(mybir.EngineType.Activation, GROUP * g, n)
                for k in range(first, n):
                    relus(g, k, e[k])
                    if live(GROUP * g + k + 2, MOE_TILES):
                        copy_rows(GROUP * g + k + 2, k % 2)
            turn(0, first=1)
            with act.Fori(1, TURNS - 1) as g:
                turn(g)
            turn(TURNS - 1, MOE_TILES - GROUP * (TURNS - 1))

        @block.vector
        def _(dve):
            count = [0]

            def link(ins):
                count[0] += 1
                ins.then_inc(s_dve, 1)
                dve.wait_ge(s_dve, count[0])

            V = nc.vector
            for g in range(4):
                dve.wait_ge(s_x[g], 16)
                for t in range(FC * g, FC * (g + 1)):
                    V.bn_stats(stats[:, t, :], X[:, t, :])
            link(V.memset(neg1[:], -1.0))
            me, se, mo, so = stats[:, :, 1], stats[:, :, 2], stats[:, :, 4], stats[:, :, 5]
            a, v, y, z = ln[:, 4, :], ln[:, 2, :], ln[:, 5, :], ln[:, 6, :]
            V.tensor_tensor(a, me, mo, ALU.add)
            V.tensor_tensor(y, me, mo, ALU.subtract)
            link(V.tensor_tensor(v, se, so, ALU.add))
            V.tensor_scalar(mean, a, 0.5, None, ALU.mult)
            link(V.scalar_tensor_tensor(y, y, 0.25, y, ALU.mult, ALU.mult))
            link(V.scalar_tensor_tensor(v, v, 1.0 / D, y, ALU.mult, ALU.add))
            V.tensor_scalar(v, v, EPS, None, ALU.add).then_inc(s_var, 1)
            dve.wait_ge(s_sqrt, 1)
            link(V.reciprocal(y, ln[:, 3, :]))
            link(V.tensor_tensor(z, y, y, ALU.mult))
            link(V.tensor_tensor(z, z, v, ALU.mult))
            link(V.tensor_scalar(z, z, -0.5, 1.5, ALU.mult, ALU.add))
            link(V.tensor_tensor(rstd, y, z, ALU.mult))

            def normalise(tile, dst):
                return V.tensor_scalar(dst, X[:, ds(tile, 1), :].rearrange("p a d -> p (a d)"),
                                       mean[:, ds(tile, 1)], rstd[:, ds(tile, 1)], ALU.subtract, ALU.mult)

            par = [0]

            def parity(b):
                return b % 2 if isinstance(b, int) else par[0]

            def rows(b):
                if live(b):
                    wait(dve, xt_done, b - 1)
                    for j in range(NJ):
                        last = normalise(b * NJ + j, XN[:, parity(b), j, :])
                    last.then_inc(xn_ready, 1)

            def lo_part(b):
                if live(b):
                    u = parity(b)
                    dve.wait_ge(xhi_ready, b + 1)
                    V.tensor_tensor(xT_lo[:, u, :], psT[:, 0:NJ * P], xT_hi[:, u, :].bitcast(f32),
                                    ALU.subtract).then_inc(xlo_ready, 1)

            def logits(g, u):
                dve.wait_ge(s_plog, g + 1)
                V.tensor_tensor(L[:, ds(g * RT, RT), :], bank[2 + u][:, 0:RT * E].rearrange("p (t e) -> p t e", e=E),
                                spread(br_sb[:].unsqueeze(1), 1, RT), ALU.add).then_inc(s_pL, 1)

            def ring_free(g):
                wait(dve, s_pT, g - 1)
                wait(dve, s_phi, g - 1)
                wait(dve, s_plo, g - 1)

            def group_rows(g, u):
                ring_free(g)
                for i in range(RT):
                    last = normalise(g * RT + i, XN[:, u, i, :])
                last.then_inc(s_pxn, 1)

            def router(g, u):
                if live(g + 1, RG):
                    group_rows(g + 1, 1 - u)
                dve.wait_ge(s_phi, g + 1)
                dve.wait_ge(s_pxn, g + 1)
                V.tensor_tensor(XS[:, 0, ds(g * RT, RT), D // 2:D].bitcast(f16), XN[:, u],
                                XS[:, 0, ds(g * RT, RT), 0:D // 2].bitcast(f16), ALU.subtract).then_inc(s_plo, 1)
                if live(g - 1):
                    logits(g - 1, 1 - u)
            dve.wait_ge(s_router_w, 32)
            dve.wait_ge(s_const, 1)
            group_rows(0, 0)
            for g in range(RG - 1):
                router(g, g % 2)
            ring_free(RG)
            rows(0)
            router(RG - 1, (RG - 1) % 2)
            ring_free(RG + 1)
            rows(1)
            lo_part(0)
            logits(RG - 1, (RG - 1) % 2)
            dve.wait_ge(s_pL, RG)

            def masked_kv(b):
                if live(b):
                    dve.wait_ge(kv_done, b + 1)
                    wait(dve, out_done, b)
                    V.tensor_tensor(BD[:], psKV, spread(bd_mask[:].unsqueeze(1), 1, NC), ALU.mult).then_inc(bd_ready, 1)

            def step(b, u, extra=None, after_lo=None, after_k=None):
                par[0] = u
                rows(b + 2)
                par[0] = 1 - u
                lo_part(b + 1)
                par[0] = u
                if after_lo:
                    after_lo()
                masked_kv(b - 1)
                if live(b):
                    for j in range(NJ):
                        dve.wait_ge(ek_ready, 2 * b + j + 1)
                        wait(dve, kv_done, b - 1)
                        V.scalar_tensor_tensor(KF[:, u, j, :], EK[:, j, :], 1.0, psK[j][:], ALU.min, ALU.max).then_inc(kf_ready, 1)
                    if after_k:
                        after_k()
                    for h in range(2):
                        dve.wait_ge(eq_ready, 2 * b + h + 1)
                        wait(dve, out_done, b - 1)
                        for c in (2 * h, 2 * h + 1):
                            last = V.scalar_tensor_tensor(QF[:, u, c, :], psQ[h][:, (c % 2) * NJ * P:(c % 2 + 1) * NJ * P],
                                                          q_bias1[:, c:c + 1], EQ[:, c, :], ALU.add, ALU.max)
                        last.then_inc(qf_ready, 1)
                        if extra and h == 0:
                            extra()
                if live(b - 1):
                    dve.wait_ge(out_done, b)
                    link2(V.tensor_scalar(den[:], psOut[:, :, HC * HD:KVW], NORM_MIN, None, ALU.max), b)
                    link2(V.reciprocal(den[:], den[:]), b)
                    wait(dve, ot_done, b - 1)
                    V.tensor_tensor(O_sb[:].rearrange("p c (h d) -> p c h d", h=HC),
                                    psOut[:, :, 0:HC * HD].rearrange("p c (h d) -> p c h d", h=HC),
                                    spread(den[:].unsqueeze(3), 3, HD), ALU.mult).then_inc(o_ready, 1)
                if live(b - 2):
                    dve.wait_ge(att_done, b - 1)
                    xb = X[:, ds((b - 2) * NJ, NJ), :]
                    V.tensor_tensor(xb, psOA[:, NJ * P:2 * NJ * P].rearrange("p (j d) -> p j d", j=NJ), xb,
                                    ALU.add).then_inc(base_ready, 1)

            def weight_maxima(i):
                for raw, m in ((W1raw, mx1), (W2raw, mx2)):
                    V.tensor_reduce(m[:, ds(i, 1)], raw[:, ds(i * 2, 2), :].rearrange("p e h -> p (e h)"), AX.X, ALU.max,
                                    apply_absolute_value=True)

            def split_weights(e):
                for raw, hi, lo, s in (
                        (W1raw[:, ds(e, 1), :].rearrange("p e (a c) -> p (e c) a", c=HCH), W1h, W1l, 0),
                        (W2raw[:, ds(e, 1), :].rearrange("p e (c a) -> p (e c) a", c=HCH), W2h, W2l, 1)):
                    dve.wait_ge(s_whi, 2 * e + 1 + s)
                    last = V.scalar_tensor_tensor(lo[:, ds(e, 1)].rearrange("p e c a -> p (e c) a"), raw,
                                                  scl[:].bitcast(f32)[:, s:s + 1],
                                                  hi[:, ds(e, 1)].rearrange("p e c a -> p (e c) a"),
                                                  ALU.mult, ALU.subtract)
                last.then_inc(s_wsplit, 1)

            def link2(ins, b):
                norm_half[0] ^= 1
                ins.then_inc(s_norm, 1)
                dve.wait_ge(s_norm, 2 * b - norm_half[0])
            norm_half = [0]

            def maxima_local():
                V.tensor_reduce(mx3[:, 0:1], mx1[:], AX.X, ALU.max)
                V.tensor_reduce(mx3[:, 1:2], mx2[:], AX.X, ALU.max)
                V.tensor_reduce(mx3[:, 2:3], b1_sb[:].rearrange("p e c -> p (e c)"), AX.X, ALU.max, apply_absolute_value=True).then_inc(s_mx, 1)

            def maxima_reduced():
                dve.wait_ge(s_mxT, 1)
                link(V.tensor_reduce(m3[0:3, :], psMaxT, AX.X, ALU.max))
                V.tensor_copy(m3b[0:3, :], spread(m3[0:3, 0:1], 1, P)).then_inc(s_m3, 1)

            def scales():
                dve.wait_ge(s_mb, 1)
                V.tensor_copy(bound[:, 1:2], psMax[:, 1:2])
                link(V.tensor_copy(c2[:], psMax[:, 2:3]))
                V.scalar_tensor_tensor(bound[:, 0:1], psMax[:, 0:1], float(D), c2[:], ALU.mult, ALU.add).then_inc(s_mread, 1)
                dve.wait_ge(s_mread, 1)
                link(V.tensor_scalar(fld[:], bound[:].bitcast(i32), 23, None, ALU.logical_shift_right))
                link(V.tensor_scalar(fld[:], fld[:], -1.0, 268.0, ALU.mult, ALU.add))
                link(V.tensor_scalar(fld[:], fld[:], 190.0, None, ALU.min))
                V.tensor_scalar(inv[:], fld[:], -1.0, 254.0, ALU.mult, ALU.add)
                link(V.tensor_scalar(scl[:], fld[:], 23, None, ALU.logical_shift_left))
                link(V.tensor_scalar(inv[:], inv[:], 23, None, ALU.logical_shift_left))
                V.tensor_tensor(c2[:], inv[:].bitcast(f32)[:, 0:1], inv[:].bitcast(f32)[:, 1:2], ALU.mult)
                V.tensor_scalar(b1s[:], b1_sb[:], scl[:].bitcast(f32)[:, 0:1], None, ALU.mult).then_inc(s_scale, 1)

            rank_b = spread(rank8[:].unsqueeze(1), 1, NT)

            def by_expert(t):
                return spread(t.unsqueeze(2), 2, E)

            def look_for(k):
                src = L2 if k else L
                link(V.tensor_reduce(top[:, k, :], src[:], AX.X, ALU.max))
                link(V.tensor_tensor(EQM[:], src[:], by_expert(top[:, k, :]), ALU.is_equal))
                link(V.tensor_tensor(EQM[:], EQM[:], rank_b, ALU.mult))

            def mark(k):
                link(V.tensor_reduce(best[:, k, :], EQM[:], AX.X, ALU.max))
                oh = ONEHOT[:, :, k, :].rearrange("p e t -> p t e")
                link(V.tensor_tensor(oh, by_expert(best[:, k, :]), rank_b, ALU.is_equal))
                if k == 0:
                    link(V.scalar_tensor_tensor(L2[:], oh, NEG, L[:], ALU.mult, ALU.add))
                else:
                    V.tensor_copy(ONEHOT16, ONEHOT.rearrange("p e k t -> p (e k t)")).then_inc(s_oneh, 1)
                    V.tensor_tensor(gtmp[:], top[:, 1, :], top[:, 0, :], ALU.subtract).then_inc(s_gd, 1)

            cinc, n, ntile, tinc, tf, cex, delta = (small[:, i, :] for i in range(7))

            def prefixes():
                dve.wait_ge(s_pfx, 1)
                link(V.tensor_tensor_scan(CUM, ones32[:], bank[0][:], 0.0, ALU.mult, ALU.add))
                V.tensor_tensor(SLOTM, CUM, bank[0][:], ALU.subtract).then_inc(s_pfxr, 1)
                dve.wait_ge(s_pfxr, 1)
                V.tensor_tensor(SLOTM, SLOTM, bank[1][:], ALU.add).then_inc(s_pfxr, 1)
                dve.wait_ge(s_pfxr, 2)

            def parts():
                V.tensor_copy(cinc, CUM.rearrange("p (e n) -> p e n", e=E)[:, :, TOPK * NT - 1])
                link(V.memset(cex[:, 0:1], 0.0))
                link(V.tensor_copy(cex[:, 1:E], cinc[:, 0:E - 1]))
                link(V.tensor_tensor(n, cinc, cex, ALU.subtract))
                link(V.tensor_scalar(smalli[:, 0, :], n, float(TS - 1), None, ALU.add))
                link(V.tensor_scalar(smalli[:, 1, :], smalli[:, 0, :], TS_LOG2, None, ALU.logical_shift_right))
                link(V.tensor_copy(ntile, smalli[:, 1, :]))
                link(V.tensor_tensor_scan(tinc, ones32[:, 0:E], ntile, 0.0, ALU.mult, ALU.add))
                link(V.tensor_tensor(tf, tinc, ntile, ALU.subtract))
                link(V.scalar_tensor_tensor(delta, tf, float(TS), cex, ALU.mult, ALU.subtract))

            def slots():
                sl = SLOTM.rearrange("p (e n) -> p e n", e=E)
                link(V.tensor_tensor(sl, sl, spread(delta.unsqueeze(2), 2, TOPK * NT), ALU.add))
                link(V.tensor_tensor(SLOTM, SLOTM, ONEHOT.rearrange("p e k t -> p (e k t)"), ALU.mult))
                link(V.tensor_reduce(slot_f[:], SLOTM.rearrange("p (e n) -> p n e", e=E), AX.X, ALU.add))
                V.tensor_copy(slot_i[:], slot_f[:]).then_inc(s_slots, 1)

            def weigh():
                dve.wait_ge(s_gexp, 1)
                link(V.tensor_scalar(best[:, 0, :], gtmp[:], 1.0, None, ALU.add))
                link(V.reciprocal(gates[:, 0, :], best[:, 0, :]))
                link(V.tensor_tensor(gates[:, 1, :], gates[:, 0, :], gtmp[:], ALU.mult))
                V.tensor_copy(XS[:, :, :, D + 1], gates[:]).then_inc(s_gates, 1)

            def tile_experts():
                link(V.tensor_tensor(ended[:], spread(tile_no[:].unsqueeze(2), 2, E),
                                     spread(tinc.unsqueeze(1), 1, ROOM), ALU.is_ge))
                link(V.tensor_reduce(expert_f[:], ended[:], AX.X, ALU.add))
                link(V.tensor_scalar(expert_i[:], expert_f[:], float(E - 1), None, ALU.min))

            def split(g, k):
                t, u = GROUP * g + k, k % 2
                dve.wait_ge(m_h, t + 1)
                wait(dve, m_down, t - 1)
                V.tensor_copy(Hs[:, u, 0, :], Hf[:, u, :]).then_inc(s_hi16, 1)
                dve.wait_ge(s_hi16, t + 1)
                V.tensor_tensor(Hs[:, u, 1, :], Hf[:, u, :], Hs[:, u, 0, :], ALU.subtract).then_inc(m_split, 1)

            look_for(0)
            mark(0)
            step(0, 0, lambda: mark(1), after_k=lambda: look_for(1))
            step(1, 1, prefixes)
            step(2, 0, lambda: (parts(), weigh()))
            step(3, 1, slots)
            dve.wait_ge(s_w, 32)
            with dve.Fori(4, 7, 2) as b:
                step(b, 0, lambda: weight_maxima(b - 4))
                step(b + 1, 1, lambda: weight_maxima(b - 3))
            step(8, 0, scales, maxima_local, maxima_reduced)
            dve.wait_ge(s_scale, 1)
            step(9, 1, lambda: (tile_experts(), split_weights(0)))
            with dve.Fori(10, 13, 2) as b:
                step(b, 0, lambda: split_weights(b - 9))
                step(b + 1, 1, lambda: split_weights(b - 8))
            step(14, 0, lambda: split_weights(5))
            step(15, 1, lambda: split_weights(7), after_k=lambda: split_weights(6))
            step(16, 0)
            step(17, 1)

            def result(g, k, e):
                t, u = GROUP * g + k, k % 2
                y = slot_tile(YT, g, k)
                dve.wait_ge(m_down, t + 1)
                V.scalar_tensor_tensor(y, bank[6 + u][:, 0:SUB * D].rearrange("p (s d) -> p s d", s=SUB),
                                       c2[:], spread(b2_sb[:, ds(e, 1), :], 1, SUB), ALU.mult, ALU.add).then_inc(m_yraw, 1)
                dve.wait_ge(m_yraw, t + 1)
                V.tensor_tensor(y, y, spread(slot_tile(SLOT_ROWS, g, k)[:, :, D + 1:D + 2], 2, D), ALU.mult).then_inc(m_y, 1)

            def turn(g, e):
                for k in range(len(e)):
                    result(g, k, e[k])
                    if live(GROUP * g + k + 2, MOE_TILES):
                        split(g, k + 2)
            split(0, 0)
            split(0, 1)
            with dve.Fori(0, TURNS - 1) as g:
                turn(g, experts(mybir.EngineType.DVE, GROUP * g, GROUP))
            first = GROUP * (TURNS - 1)
            turn(TURNS - 1, experts(mybir.EngineType.DVE, first, MOE_TILES - first))

            for g in range(OUT_CHUNKS):
                dve.wait_ge(s_yb[g], 32)
                at = slice(OC * g, OC * (g + 1))
                V.tensor_tensor(X[:, at, :], X[:, at, :], YB[:, 0, at, :], ALU.add).then_inc(s_comb, 1)
                dve.wait_ge(s_comb, g + 1)
                V.tensor_tensor(X[:, at, :], X[:, at, :], YB[:, 1, at, :], ALU.add).then_inc(s_fin, 1)

        @block.tensor
        def _(pe):
            mm = nc.tensor.matmul

            def three(ps, a_hi, a_lo, b_hi, b_lo, first=True, last=True):
                mm(ps, a_lo, b_hi, start=first, stop=False)
                mm(ps, a_hi, b_lo, start=False, stop=False)
                return mm(ps, a_hi, b_hi, start=False, stop=last)

            pe.wait_ge(s_const, 1)
            pe.wait_ge(s_early, 16 * 8)
            nc.tensor.transpose(bank[3][:, 0:P], Wq_sb[:], ident[:])
            nc.tensor.transpose(bank[3][:, P:2 * P], Wk_sb[:], ident[:]).then_inc(s_wt, 1)
            pe.wait_ge(s_rb, 1)
            pe.wait_ge(s_wtc, 1)
            mm(bank[4][:], WT[:, 0:P], RB, start=True, stop=True)
            mm(bank[5][:], WT[:, P:2 * P], RB, start=True, stop=True).then_inc(s_fold, 1)

            pe.wait_ge(s_router_w, 32)

            def transposes(g, u):
                pe.wait_ge(s_pxn, g + 1)
                wait(pe, s_pxT, g - 1)
                for i in range(RT):
                    last = nc.tensor.transpose(bank[u][:, i * P:(i + 1) * P], XN[:, u, i, :], ident[:])
                last.then_inc(s_pT, 1)

            def router(g, u):
                if live(g + 1, RG):
                    transposes(g + 1, 1 - u)
                pe.wait_ge(s_pxT, g + 1)
                wait(pe, s_pL, g - 1)
                for i in range(RT):
                    last = mm(bank[2 + u][:, i * E:(i + 1) * E], XTR[:, u, i * P:(i + 1) * P], Wr_sb[:], start=True, stop=True)
                last.then_inc(s_plog, 1)
            transposes(0, 0)
            router(0, 0)
            mm(bank[7][:], BK_REP, RB, start=True, stop=True)
            for c in range(NC):
                last = mm(bank[6][:, c:c + 1], RB[:, c * P:(c + 1) * P], bqk_sb[:, 0:1], start=True, stop=True)
            last.then_inc(s_fold, 1)
            for g in range(1, RG - 1):
                router(g, g % 2)

            def passes(ps, *pairs):
                for n, (a, b) in enumerate(pairs):
                    yield lambda a=a, b=b, n=n: mm(ps, a, b, start=(n == 0), stop=(n == len(pairs) - 1))

            def kproj(j, u):
                at = slice(j * P, (j + 1) * P)
                hi, lo = xT_hi[:, u, at], xT_lo[:, u, at]
                return passes(psK[j][:], (pick3[:], BIAS3[:, 0:FEAT]), (lo, WkR_hi[:]), (hi, WkR_lo[:]), (hi, WkR_hi[:]))

            def qproj(c, u):
                at = slice(c * P, (c + 1) * P)
                return passes(psQ[c // 2][:, (c % 2) * NJ * P:(c % 2 + 1) * NJ * P], (WqR_lo[:, at], xT_hi[:, u, :]),
                              (WqR_hi[:, at], xT_lo[:, u, :]), (WqR_hi[:, at], xT_hi[:, u, :]))

            def step(b, u, before_q=None, before_out=None, after_kv=None):
                if live(b + 1):
                    pe.wait_ge(xn_ready, b + 2)
                    wait(pe, xlo_ready, b + 1)
                    wait(pe, xhi_ready, b + 1)
                    for j in range(NJ):
                        last = nc.tensor.transpose(psT[:, j * P:(j + 1) * P], XN[:, 1 - u, j, :], ident[:])
                    last.then_inc(xt_done, 1)
                if live(b):
                    pe.wait_ge(xhi_ready, b + 1)
                    pe.wait_ge(xlo_ready, b + 1)
                if live(b - 1):
                    pe.wait_ge(v_ready, b)
                    pe.wait_ge(kf_ready, 2 * b)
                for j in range(NJ):
                    wide = kproj(j, u) if live(b) else iter(())
                    for c in range(NC):
                        if live(b):
                            last = next(wide)()
                            if c == NC - 1:
                                last.then_inc(k_done, 1)
                        if live(b - 1):
                            ch, i = 2 * j + c // 2, c % 2
                            last = mm(psKV[:, ch, :], KF[:, 1 - u, i, ch * P:(ch + 1) * P], VA[:, 1 - u, i, ch, :],
                                      start=(i == 0), stop=(i == NJ - 1))
                            if j == NJ - 1 and c == NC - 1:
                                last.then_inc(kv_done, 1)
                if after_kv:
                    after_kv()
                if live(b - 2):
                    pe.wait_ge(o_ready, b - 1)
                    wait(pe, base_ready, b - 2)
                    ov = O_sb[:].rearrange("p c w -> p (c w)")
                    for j in range(NJ):
                        last = nc.tensor.transpose(psOA[:, j * P:(j + 1) * P], ov[:, j * P:(j + 1) * P], ident[:])
                    last.then_inc(ot_done, 1)
                if before_q:
                    before_q()
                if live(b):
                    wait(pe, qf_ready, 2 * b - 1)
                    for c in range(2):
                        for product in qproj(c, u):
                            last = product()
                    last.then_inc(q_done, 1)
                    wait(pe, bd_ready, b)
                    for j in range(NJ):
                        at, to = slice(j * P, (j + 1) * P), psV[:, j * D:(j + 1) * D]
                        mm(to, pick3[:], BIAS3[:, FEAT:FEAT + D], start=True, stop=False)
                        last = three(to, xT_hi[:, u, at], xT_lo[:, u, at], Wv_hi[:], Wv_lo[:], first=False)
                    last.then_inc(v_done, 1)
                    wait(pe, qf_ready, 2 * b)
                if before_out:
                    before_out()
                if live(b - 1):
                    pe.wait_ge(bd_ready, b)
                    pe.wait_ge(qf_ready, 2 * b)
                    wait(pe, o_ready, b - 1)
                wide = [p for c in (2, 3) for p in qproj(c, u)] if live(b) else []
                for n in range(NJ * NC):
                    if n < len(wide):
                        last = wide[n]()
                        if n == len(wide) - 1:
                            last.then_inc(q_done, 1)
                    if live(b - 1):
                        j, c = n // NC, n % NC
                        last = mm(psOut[:, n, :], QF[:, 1 - u, c, j * P:(j + 1) * P], BD[:, c, :], start=True, stop=True)
                        if n == NJ * NC - 1:
                            last.then_inc(out_done, 1)
                if live(b - 2):
                    pe.wait_ge(ot_ready, b - 1)
                    for j in range(NJ):
                        to = psOA[:, (NJ + j) * P:(NJ + j + 1) * P]
                        mm(to, pick3[:], BIAS3[:, FEAT + D:NBIAS], start=True, stop=False)
                        last = mm(to, OT_sb[:, j * P:(j + 1) * P], Wo_sb[:], start=False, stop=True)
                    last.then_inc(att_done, 1)

            def transpose_maxima():
                pe.wait_ge(s_mx, 1)
                pe.wait_ge(xhi_ready, 10)
                pe.wait_ge(xlo_ready, 10)
                nc.tensor.transpose(psMaxT, mx3[:], ident[:]).then_inc(s_mxT, 1)

            def broadcast_maxima():
                pe.wait_ge(s_m3, 1)
                mm(psMax, m3b[0:3, :], ident[0:3, 0:3], start=True, stop=True).then_inc(s_mb, 1)

            def prefix_sums():
                pe.wait_ge(s_oneh, 1)
                pe.wait_ge(xhi_ready, 3)
                pe.wait_ge(xlo_ready, 3)
                mm(bank[1][:], upper[:], ONEHOT16, start=True, stop=True)
                mm(bank[0][:], ones[:], ONEHOT16, start=True, stop=True).then_inc(s_pfx, 1)

            pe.wait_ge(s_pxT, RG - 1)
            step(-1, 1)
            router(RG - 1, (RG - 1) % 2)
            pe.wait_ge(s_pL, RG)
            pe.wait_ge(s_bias, 1)
            pe.wait_ge(s_late, 16 * 3)
            step(0, 0)
            step(1, 1, before_out=prefix_sums)
            pe.wait_ge(s_pfxr, 1)
            step(2, 0)
            step(3, 1)
            steps(pe, 4, 7, step)
            step(8, 0, transpose_maxima, broadcast_maxima)
            pe.wait_ge(s_mread, 1)
            step(9, 1)
            steps(pe, 10, 13, step)
            step(14, 0)
            step(15, 1)
            words = SLOT_ROWS[:].bitcast(f16)

            def rows(g, k):
                t, u = GROUP * g + k, k % 2
                wait(pe, m_xT, t - 1)
                for part in range(2):
                    for i in range(SUB):
                        at = (part * SUB + i) * P // 2
                        last = nc.tensor.transpose(
                            rows_bank(t, u)[:, at:at + P // 2].bitcast(f16),
                            slot_tile(words, g, k, i, 1)[:, :, part * D:(part + 1) * D].rearrange("p a d -> p (a d)"), identh[:])
                last.then_inc(m_T, 1)

            def up(g, k, e):
                t, u = GROUP * g + k, k % 2
                pe.wait_ge(m_xT, t + 1)
                wait(pe, m_h, t - 1)
                xh = XTS[:, u, 0:TS // 2].bitcast(f16)
                xl = XTS[:, u, TS // 2:TS].bitcast(f16)
                for c in range(HCH):
                    to, hi, lo = up_bank(u, c), weights(W1h, e, c), weights(W1l, e, c)
                    mm(to, lo, xh, start=True, stop=False)
                    mm(to, hi, xl, start=False, stop=False)
                    last = mm(to, hi, xh, start=False, stop=True)
                last.then_inc(m_up, 1)

            def down(g, k, e):
                t, u = GROUP * g + k, k % 2
                pe.wait_ge(m_split, t + 1)
                wait(pe, m_y, t - 1)
                for i in range(SUB):
                    to = bank[6 + u][:, i * D:(i + 1) * D]
                    for c in range(HCH):
                        hi, lo = weights(W2h, e, c), weights(W2l, e, c)
                        rows_at = slice(c * TS + i * P, c * TS + (i + 1) * P)
                        hh, hl = Hs[:, u, 0, rows_at], Hs[:, u, 1, rows_at]
                        mm(to, hl, hi, start=(c == 0), stop=False)
                        mm(to, hh, lo, start=False, stop=False)
                        last = mm(to, hh, hi, start=False, stop=(c == HCH - 1))
                last.then_inc(m_down, 1)

            def weights(v, e, c):
                return v[:, ds(e, 1), c, :].rearrange("p a n -> p (a n)")

            pe.wait_ge(s_load, 16)
            pe.wait_ge(xhi_ready, NBATCH)
            pe.wait_ge(xlo_ready, NBATCH)
            rows(0, 0)
            e = experts(mybir.EngineType.PE, 0, GROUP + 1)
            pe.wait_ge(s_wsplit, E)
            step(16, 0, after_kv=lambda: up(0, 0, e[0]))
            rows(0, 1)
            step(17, 1, lambda: (rows(0, 2), up(0, 1, e[1])))

            def turn(g, e, n=GROUP, first=1):
                for k in range(first, n + 1):
                    t = GROUP * g + k
                    if live(t + 1, MOE_TILES):
                        rows(g, k + 1)
                    if live(t, MOE_TILES):
                        up(g, k, e[k + 1])
                    if live(t - 2, MOE_TILES):
                        down(g, k - 2, e[k - 1])

            pe.wait_ge(base_ready, NBATCH)
            turn(0, [None] + e, first=2)
            with pe.Fori(1, TURNS - 1) as g:
                turn(g, experts(mybir.EngineType.PE, GROUP * g - 1, GROUP + 2))
            first = GROUP * (TURNS - 1) - 1
            e = experts(mybir.EngineType.PE, first, MOE_TILES - first)
            turn(TURNS - 1, e + [None] * 2, MOE_TILES - first)


_INS = ["L0_attn_x", "L0_attn_Wq", "L0_attn_bq", "L0_attn_Wk", "L0_attn_bk", "L0_attn_Wv", "L0_attn_bv",
        "L0_attn_Wo", "L0_attn_bo", "L0_attn_random_matrix", "L0_ffn_Wr", "L0_ffn_br", "L0_ffn_W1",
        "L0_ffn_b1", "L0_ffn_W2", "L0_ffn_b2"]


def kernel(**inputs):
    import numpy as _np
    import concourse.bacc as _bacc
    from concourse import mybir as _mybir
    from concourse.bass_utils import run_bass_kernel_spmd as _run

    nc = _bacc.Bacc("TRN2", target_bir_lowering=False, num_devices=1)
    arrays, args = {}, []
    for name in _INS:
        a = _np.ascontiguousarray(inputs[name])
        arrays[f"in_{name}"] = a
        args.append(nc.dram_tensor(f"in_{name}", a.shape, _mybir.dt.from_np(a.dtype), kind="ExternalInput").ap())
    f32 = _mybir.dt.float32
    out = nc.dram_tensor("out_0", (NBATCH, NJ * P, D), f32, kind="ExternalOutput").ap()
    rows_dram = nc.dram_tensor("slot_rows", (SLOTS, ROWW), f32, kind="Internal").ap()
    y_dram = nc.dram_tensor("expert_results", (TOPK * T, D), f32, kind="Internal").ap()
    program(nc, *args, out, rows_dram, y_dram)
    r = _run(nc, [arrays], core_ids=[0])
    return r.results[0]["out_0"]
```
